# Optimizing a Trainium2 kernel written in Bass

```python
import numpy as np
import jax
import jax.numpy as jnp

def _softmax(x, axis=-1):
    return jax.nn.softmax(x, axis=axis)

def _gelu(x):
    return jax.nn.gelu(x, approximate=True)

def _silu(x):
    return jax.nn.silu(x)

def _sigmoid(x):
    return jax.nn.sigmoid(x)

def _layernorm(x, axis=-1, eps=1e-05):
    m = jnp.mean(x, axis=axis, keepdims=True)
    v = jnp.var(x, axis=axis, keepdims=True)
    return (x - m) / jnp.sqrt(v + eps)

def _scatter_add(tgt, idx, src, axis=0):
    return tgt.at[idx].add(src)

def _segment_sum(src, seg, n):
    return jax.ops.segment_sum(src, seg, n)
kernel_name = 'mk_flamingo_gated_d1_seqx_r4_4fb9d1'

def setup_inputs(seed: int=0):
    np.random.seed(seed)
    _w = jnp.asarray

    def _rec_inputs():
        import jax
        import jax.numpy as jnp
        _rk = jax.random.key(seed)
        x = -0.0002928 + 1 * jax.random.normal(jax.random.fold_in(_rk, 1), (4, 1024, 256), jnp.float32)
        _lenS = 1024 - jax.random.randint(jax.random.fold_in(_rk, 7), (4,), 0, max(1, 1024 // 4) + 1, jnp.int32)
        _lenS2 = 154 - jax.random.randint(jax.random.fold_in(_rk, 8), (4,), 0, max(1, 154 // 4) + 1, jnp.int32)
        _ctx_1024P = jax.random.normal(jax.random.fold_in(_rk, 11), (4, 16, 256), jnp.float32)
        _ctx_1024c = jax.random.dirichlet(jax.random.fold_in(_rk, 511), 0.3 * jnp.ones((16,), jnp.float32), (4, 154))
        _ctx_1024t = jnp.einsum('bsk,bkd->bsd', _ctx_1024c, _ctx_1024P)
        _ctx_1024t = _ctx_1024t * jax.lax.rsqrt(jnp.mean(jnp.square(_ctx_1024t)) + 1e-12) * 0.953939
        ctx_1024 = 4.13588e-05 + 0.999923 * (_ctx_1024t + 0.3 * jax.random.normal(jax.random.fold_in(_rk, 611), (4, 154, 256), jnp.float32))
        _validS = jnp.arange(1024)[None, :] < _lenS[:, None]
        _validS2 = jnp.arange(154)[None, :] < _lenS2[:, None]
        _causal = jnp.tril(jnp.ones((1024, 1024), dtype=bool))
        mask_BxS2_bk0 = jnp.logical_not(jnp.broadcast_to(_validS2[:, :], (4, 154)))
        _g = jax.random.normal(jax.random.fold_in(_rk, 9001), (2, 1), jnp.float32)
        _g = jnp.sign(_g) * jnp.maximum(jnp.abs(_g), 1.0) + (_g == 0) * 1.0
        g_xattn = _g[0]
        g_ffn = _g[1]
        return (x, ctx_1024, mask_BxS2_bk0, g_xattn, g_ffn)
    x, ctx_1024, mask_BxS2_bk0, g_xattn, g_ffn = _rec_inputs()

    def _L0_xattn_setup():
        import jax, jax.numpy as jnp
        import numpy as np
        D_MODEL = 256
        N_HEAD = 16
        D_H = D_MODEL // N_HEAD
        key = jax.random.key(seed)
        ks = jax.random.split(key, 12)
        B, LQ, LK = (4, 256, 512)
        s = 1.0 / np.sqrt(D_MODEL)
        inp = {'q_input': jax.random.normal(ks[0], (B, LQ, D_MODEL), jnp.float32), 'kv_input': jax.random.normal(ks[1], (B, LK, D_MODEL), jnp.float32), 'key_padding_mask': jax.random.randint(ks[2], (B, LK), 0, 2) > 0, 'W_Q': jax.random.normal(ks[3], (D_MODEL, D_MODEL), jnp.float32) * s, 'b_Q': jnp.zeros((D_MODEL,), jnp.float32), 'W_K': jax.random.normal(ks[4], (D_MODEL, D_MODEL), jnp.float32) * s, 'b_K': jnp.zeros((D_MODEL,), jnp.float32), 'W_V': jax.random.normal(ks[5], (D_MODEL, D_MODEL), jnp.float32) * s, 'b_V': jnp.zeros((D_MODEL,), jnp.float32), 'W_O': jax.random.normal(ks[6], (D_MODEL, D_MODEL), jnp.float32) * s, 'b_O': jnp.zeros((D_MODEL,), jnp.float32)}
        return inp
    _L0_xattn_all = _L0_xattn_setup()
    _L0_xattn_in = {k: v for k, v in _L0_xattn_all.items() if k in ('W_Q', 'b_Q', 'W_K', 'b_K', 'W_V', 'b_V', 'W_O', 'b_O')}
    del _L0_xattn_all

    def _L0_ffn_setup():
        import jax, jax.numpy as jnp
        import numpy as np
        DIM = 256
        HIDDEN = 768
        SCALE = 1.0 / 127.0

        def _dequant(w_int, dtype):
            return w_int.astype(dtype) * jnp.asarray(SCALE, dtype)
        key = jax.random.key(seed)
        k_x, k_g, k_u, k_d = jax.random.split(key, 4)
        x = jax.random.normal(k_x, (4, 512, DIM), dtype=jnp.float32)
        w_gate = jax.random.randint(k_g, (HIDDEN, DIM), -127, 128, dtype=jnp.int32)
        w_up = jax.random.randint(k_u, (HIDDEN, DIM), -127, 128, dtype=jnp.int32)
        w_down = jax.random.randint(k_d, (DIM, HIDDEN), -127, 128, dtype=jnp.int32)
        return {'x': x, 'w_gate': w_gate, 'w_up': w_up, 'w_down': w_down}
    _L0_ffn_all = _L0_ffn_setup()
    _L0_ffn_in = {k: v for k, v in _L0_ffn_all.items() if k in ('w_gate', 'w_up', 'w_down')}
    del _L0_ffn_all
    return {'x': x, 'ctx_1024': ctx_1024, 'mask_BxS2_bk0': mask_BxS2_bk0, 'g_xattn': g_xattn, 'g_ffn': g_ffn, 'L0_xattn_W_Q': _L0_xattn_in['W_Q'], 'L0_xattn_b_Q': _L0_xattn_in['b_Q'], 'L0_xattn_W_K': _L0_xattn_in['W_K'], 'L0_xattn_b_K': _L0_xattn_in['b_K'], 'L0_xattn_W_V': _L0_xattn_in['W_V'], 'L0_xattn_b_V': _L0_xattn_in['b_V'], 'L0_xattn_W_O': _L0_xattn_in['W_O'], 'L0_xattn_b_O': _L0_xattn_in['b_O'], 'L0_ffn_w_gate': _L0_ffn_in['w_gate'], 'L0_ffn_w_up': _L0_ffn_in['w_up'], 'L0_ffn_w_down': _L0_ffn_in['w_down']}

def reference(x, ctx_1024, mask_BxS2_bk0, g_xattn, g_ffn, L0_xattn_W_Q, L0_xattn_b_Q, L0_xattn_W_K, L0_xattn_b_K, L0_xattn_W_V, L0_xattn_b_V, L0_xattn_W_O, L0_xattn_b_O, L0_ffn_w_gate, L0_ffn_w_up, L0_ffn_w_down):
    import jax
    import jax.numpy as jnp

    def _L0_xattn_ref(q_input, kv_input, key_padding_mask, W_Q, b_Q, W_K, b_K, W_V, b_V, W_O, b_O):
        import jax, jax.numpy as jnp
        import numpy as np
        D_MODEL = 256
        N_HEAD = 16
        D_H = D_MODEL // N_HEAD
        B, LQ, _ = q_input.shape
        LK = kv_input.shape[1]
        q = q_input @ W_Q + b_Q
        k = kv_input @ W_K + b_K
        v = kv_input @ W_V + b_V
        q = q.reshape(B, LQ, N_HEAD, D_H).transpose(0, 2, 1, 3)
        k = k.reshape(B, LK, N_HEAD, D_H).transpose(0, 2, 1, 3)
        v = v.reshape(B, LK, N_HEAD, D_H).transpose(0, 2, 1, 3)
        sim = jnp.einsum('bhqd,bhkd->bhqk', q, k) / jnp.sqrt(jnp.float32(D_H))
        neg_inf = jnp.finfo(sim.dtype).min
        mask = key_padding_mask[:, None, None, :]
        sim = jnp.where(mask, neg_inf, sim)
        attn = jax.nn.softmax(sim, axis=-1)
        out = jnp.einsum('bhqk,bhkd->bhqd', attn, v)
        out = out.transpose(0, 2, 1, 3).reshape(B, LQ, D_MODEL)
        return out @ W_O + b_O

    def _L0_ffn_ref(x, w_gate, w_up, w_down):
        import jax, jax.numpy as jnp
        import numpy as np
        DIM = 256
        HIDDEN = 768
        SCALE = 1.0 / 127.0

        def _dequant(w_int, dtype):
            return w_int.astype(dtype) * jnp.asarray(SCALE, dtype)
        wg = _dequant(w_gate, x.dtype)
        wu = _dequant(w_up, x.dtype)
        wd = _dequant(w_down, x.dtype)
        gate = jnp.einsum('bsd,hd->bsh', x, wg)
        up = jnp.einsum('bsd,hd->bsh', x, wu)
        h = jax.nn.silu(gate) * up
        return jnp.einsum('bsh,dh->bsd', h, wd)
    x = x + jnp.tanh(g_xattn[0]) * _L0_xattn_ref(_layernorm(x, axis=-1), ctx_1024, mask_BxS2_bk0, L0_xattn_W_Q, L0_xattn_b_Q, L0_xattn_W_K, L0_xattn_b_K, L0_xattn_W_V, L0_xattn_b_V, L0_xattn_W_O, L0_xattn_b_O)
    x = x + jnp.tanh(g_ffn[0]) * _L0_ffn_ref(_layernorm(x, axis=-1), L0_ffn_w_gate, L0_ffn_w_up, L0_ffn_w_down)
    return x

_drawn_inputs = setup_inputs


def setup_inputs(seed=0):
    import zlib

    import numpy as np

    out = dict(_drawn_inputs(seed))
    spreads = {'L0_xattn_b_Q': (0.0, 0.361),
     'L0_xattn_b_K': (0.0, 0.8),
     'L0_xattn_b_V': (0.0, 0.1),
     'L0_xattn_b_O': (0.0, 0.1)}
    factors = {}
    for name, (base, spread) in spreads.items():
        noise = np.random.default_rng([zlib.crc32(name.encode()), seed]).standard_normal(out[name].shape)
        drawn = base * np.exp(spread * noise) if base else spread * noise
        out[name] = jnp.asarray(drawn.astype(out[name].dtype))
    for name, factor in factors.items():
        out[name] = (out[name] * factor).astype(out[name].dtype)
    return out
```

```python
from contextlib import ExitStack

import concourse.bass as bass
from concourse import mybir

ALU = mybir.AluOpType
ACT = mybir.ActivationFunctionType
AX = mybir.AxisListType
F32 = mybir.dt.float32
F16 = mybir.dt.float16
I32 = mybir.dt.int32
U8 = mybir.dt.uint8

P = 128
EPS = 1e-5
WEIGHT_SCALE = 1.0 / 127.0

BATCH, SEQ, DIM = 4, 1024, 256
KEYS = 154
HEADS = 16
DH = DIM // HEADS
HIDDEN = 768

CHUNK = 512
TILES = CHUNK // P
CHUNKS = BATCH * SEQ // CHUNK
PER_BATCH = SEQ // CHUNK
DT = DIM // P
HT = HIDDEN // P
PAIRS = HEADS // 2
GROUPS = PAIRS // 2
PAIR_KEYS = 2 * KEYS
ROWS = 103
TILE_ROWS = [ROWS, ROWS, PAIR_KEYS - 2 * ROWS]
SPLIT = KEYS - ROWS
ST_PER_GROUP = 2 * len(TILE_ROWS)
ST_PER_CHUNK = GROUPS * ST_PER_GROUP
PV_PARTS = [(0, 0), (1, 1), (1, 0), (2, 1)]

QK_SCALE = 16.0
MASK_ROW = 3 * 32
MAX_ROW = MASK_ROW + 1
STACK_ROWS = MAX_ROW + 2
MASK_ONE = 32768.0
MAX_UNIT = 4096.0
EXP_SCALE = 1.0 / (QK_SCALE * QK_SCALE * DH ** 0.5)

STACK_DMAS = 3 * 4


def flamingo_block(nc, x, ctx_t, mask, g_xattn, g_ffn, w_q, b_q, w_k, b_k, w_v, b_v, w_o, b_o,
                   w_gate_t, w_up_t, w_down_t, out):
    x_rows = x.rearrange("b (n p) d -> p (b n) d", p=P)
    out_rows = out.rearrange("b (n p) d -> p (b n) d", p=P)

    with ExitStack() as ctx:
        def sb(name, shape, dtype=F32, stack=ctx):
            return stack.enter_context(nc.sbuf_tensor(name, shape, dtype))

        def sem(name, stack=ctx):
            return stack.enter_context(nc.semaphore(name))

        x_sb = sb("x_sb", [P, CHUNKS * TILES, DIM])
        ident = sb("ident", [P, P])
        ffn_gate = sb("ffn_gate", [P, 1])
        wi_gu = sb("wi_gu", [P, DT, 2, HIDDEN], I32)
        wi_d = sb("wi_d", [P, HT, DIM], I32)
        stats = sb("stats", [P, TILES, 6])
        mean_var = sb("mean_var", [P, TILES, 2])
        var_eps = sb("var_eps", [P, TILES])
        minus_half = sb("minus_half", [P, TILES])
        eps = sb("eps", [P, TILES])
        rstd = sb("rstd", [P, TILES])
        xh = sb("xh", [P, TILES, DIM])
        xh_t = sb("xh_t", [P, DT, CHUNK])
        weights_loaded = sem("weights_loaded")

        with ExitStack() as att_stack:
            attention(nc, att_stack, sb, sem, x_rows, x_sb, ident, ffn_gate, wi_gu, wi_d, stats,
                      mean_var, var_eps, eps, minus_half, rstd, xh, xh_t, weights_loaded,
                      ctx_t, mask, g_xattn, g_ffn, w_q, b_q, w_k, b_k, w_v, b_v, w_o, b_o,
                      w_gate_t, w_up_t, w_down_t)
        with ExitStack() as ffn_stack:
            feed_forward(nc, ffn_stack, sb, sem, out_rows, x_sb, ident, ffn_gate, wi_gu, wi_d, stats,
                         mean_var, var_eps, eps, minus_half, rstd, xh, xh_t, weights_loaded)


def first(n):
    return isinstance(n, int) and n == 0


def inverse_deviation(pool, n, stats_done, pool_step, var_eps, mean_var, eps, minus_half, rstd):
    pool.wait_ge(stats_done, n + 1)
    pool.tensor_tensor(var_eps[:], mean_var[:, :, 1], eps[:], ALU.add).then_inc(pool_step, 1)
    pool.wait_ge(pool_step, 2 * n + 1)
    pool.tensor_tensor(rstd[:], var_eps[:], minus_half[:], ALU.pow).then_inc(pool_step, 1)


def row_stats(dve, n, x_sb, stats, mean_var, stats_step, stats_done, normed, waiter):
    if not first(n):
        dve.wait_ge(normed, n)
    for t in range(TILES):
        last = dve.bn_stats(stats[:, t, :], x_sb[:, TILES * n + t, :])
    last.then_inc(stats_step, 1)
    dve.wait_ge(stats_step, n + 1)
    dve.tensor_copy(waiter[:], stats[:, 0, 0:1])
    for t in range(TILES):
        last = dve.bn_aggr(mean_var[:, t, :], stats[:, t, :])
    last.then_inc(stats_done, 1)


def normalise_rows(dve, n, x_sb, xh, mean_var, rstd, pool_step, xt_psum, normed):
    dve.wait_ge(pool_step, 2 * n + 2)
    if not first(n):
        dve.wait_ge(xt_psum, DT * n)
    for t in range(TILES):
        last = dve.tensor_scalar(xh[:, t, :], x_sb[:, TILES * n + t, :], mean_var[:, t, 0:1],
                                 rstd[:, t:t + 1], ALU.subtract, ALU.mult)
    last.then_inc(normed, 1)


def attention(nc, st, sb, sem, x_rows, x_sb, ident, ffn_gate, wi_gu, wi_d, stats, mean_var, var_eps,
              eps, minus_half, rstd, xh, xh_t, weights_loaded, ctx_t, mask, g_xattn, g_ffn,
              w_q, b_q, w_k, b_k, w_v, b_v, w_o, b_o, w_gate_t, w_up_t, w_down_t):
    def a_sb(name, shape, dtype=F32):
        return sb(name, shape, dtype, st)

    def a_sem(name):
        return sem(name, st)

    wq = a_sb("wq", [P, DT, DIM])
    wk = a_sb("wk", [P, DT, DIM])
    wv = a_sb("wv", [P, DT, DIM])
    wo = a_sb("wo", [P, DT, DIM])
    bq = a_sb("bq", [P, DT])
    bk = a_sb("bk", [P, DT])
    bv = a_sb("bv", [P, DIM])
    bo = a_sb("bo", [P, DIM])
    gates = a_sb("gates", [P, 2])
    att_gate = a_sb("att_gate", [P, 1])
    ctx2 = a_sb("ctx2", [P, DT, BATCH, 2, KEYS])
    mask_u8 = a_sb("mask_u8", [P, BATCH, KEYS], U8)
    mask_f = a_sb("mask_f", [P, BATCH, KEYS])
    some_valid = a_sb("some_valid", [P, BATCH])
    mask_row = a_sb("mask_row", [P, BATCH, KEYS], F16)
    mask_ones = a_sb("mask_ones", [P, CHUNK], F16)
    unit_row = a_sb("unit_row", [P, KEYS], F16)
    k_f = a_sb("k_f", [P, DT, BATCH, KEYS])
    k_hi = a_sb("k_hi", [P, DT, BATCH, KEYS], F16)
    k_lo = a_sb("k_lo", [P, DT, BATCH, KEYS], F16)
    k_stack = a_sb("k_stack", [P, BATCH, PAIRS, PAIR_KEYS], F16)
    v_all = a_sb("v_all", [P, BATCH, PAIRS, 4, 2, DH])
    v_cur = a_sb("v_cur", [P, PAIRS, 4, 2, DH])
    v_mid = a_sb("v_mid", [P, DIM])
    head_rows = a_sb("head_rows", [P, 2])
    q_hi = a_sb("q_hi", [P, DT, CHUNK], F16)
    q_lo = a_sb("q_lo", [P, DT, CHUNK], F16)
    q_stack = a_sb("q_stack", [P, 2, PAIRS, CHUNK], F16)
    waiter = a_sb("waiter", [P, 1])
    neg_max = a_sb("neg_max", [P, TILES, HEADS])
    neg_max_t = a_sb("neg_max_t", [HEADS, CHUNK], F16)
    probs = a_sb("probs", [P, 2 * ST_PER_GROUP, CHUNK])
    ou = a_sb("ou", [P, 2, CHUNK])
    rec = a_sb("rec", [P, 2, TILES, 4])
    att = a_sb("att", [P, TILES, DIM])
    att_t = a_sb("att_t", [P, DT, CHUNK])

    def bank(name):
        return st.enter_context(nc.psum_tensor(name, [P, 512], F32))

    work = [bank(f"work{i}") for i in range(2)]
    mx_bank = [bank(f"mx_bank{i}") for i in range(2)]
    st_bank = [bank(f"st_bank{i}") for i in range(2)]
    pv_bank = [bank(f"pv_bank{i}") for i in range(2)]

    att_params = a_sem("att_params")
    x_first = a_sem("x_first")
    x_rest = a_sem("x_rest")
    pool_init = a_sem("pool_init")
    params_ready = a_sem("params_ready")
    gates_tanh = a_sem("gates_tanh")
    mask_step = a_sem("mask_step")
    k_psum = a_sem("k_psum")
    k_step = a_sem("k_step")
    k_split = a_sem("k_split")
    v_psum = a_sem("v_psum")
    v_step = a_sem("v_step")
    v_done = a_sem("v_done")
    k_stacked = a_sem("k_stacked")
    stats_done = a_sem("stats_done")
    stats_step = a_sem("stats_step")
    pool_step = a_sem("pool_step")
    normed = a_sem("normed")
    residual_ready = a_sem("residual_ready")
    xt_psum = a_sem("xt_psum")
    xt_sb = a_sem("xt_sb")
    q_psum = a_sem("q_psum")
    q_hi_done = a_sem("q_hi_done")
    q_lo_done = a_sem("q_lo_done")
    q_stacked = a_sem("q_stacked")
    mx_psum = a_sem("mx_psum")
    mx_reduced = a_sem("mx_reduced")
    mxt_psum = a_sem("mxt_psum")
    mxt_sb = a_sem("mxt_sb")
    max_stacked = a_sem("max_stacked")
    st_psum = a_sem("st_psum")
    exp_done = a_sem("exp_done")
    v_ready = [a_sem(f"v_ready{g}") for g in range(GROUPS)]
    pv_psum = a_sem("pv_psum")
    pv_sb = a_sem("pv_sb")
    nt_psum = a_sem("nt_psum")
    rec_done = a_sem("rec_done")
    att_done = a_sem("att_done")
    at_psum = a_sem("at_psum")
    at_sb = a_sem("at_sb")
    o_psum = a_sem("o_psum")
    x1_done = a_sem("x1_done")

    MX = TILES * PAIRS
    CREDIT = {"mx_reduced": 2, "exp_done": 2, "pv_psum": 2, "pv_sb": 2, "nt_psum": 2, "at_psum": DT,
              "o_psum": 2, "x1_done": 2}

    def all_chunks(engine, chunk):
        with engine.Fori(0, BATCH - 1) as b:
            for j in range(PER_BATCH):
                chunk(b * PER_BATCH + j, b, j, True, True)
        for j in range(PER_BATCH):
            chunk((BATCH - 1) * PER_BATCH + j, BATCH - 1, j, j < PER_BATCH - 1, False)

    with nc.Block() as block:

        @block.sync
        def _(sp):
            sp.dma_start(x_sb[:, 0:TILES, :], x_rows[:, 0:TILES, :]).then_inc(x_first, 16)
            rows = lambda w: w.rearrange("(t p) n -> p t n", p=P)
            wide = lambda b: b.rearrange("(a n) -> a n", a=1)
            loads = [(ctx2[:, :, :, i, :], rows(ctx_t).rearrange("p t (b k) -> p t b k", b=BATCH)) for i in range(2)]
            loads += [
                (wq[:], rows(w_q)), (wk[:], rows(w_k)), (wv[:], rows(w_v)), (wo[:], rows(w_o)),
                (bq[:], b_q), (bk[:], b_k),
                (bv[:], wide(b_v).broadcast_to([P, DIM])), (bo[:], wide(b_o).broadcast_to([P, DIM])),
                (gates[:, 0:1], wide(g_xattn).broadcast_to([P, 1])), (gates[:, 1:2], wide(g_ffn).broadcast_to([P, 1])),
                (mask_u8[:], mask.unsqueeze(0).broadcast_to([P, BATCH, KEYS])),
            ]
            split = []
            for dst, src in loads:
                if len(dst.shape) == 4:
                    split += [(dst[:, t], src[:, t]) for t in range(DT)]
                else:
                    split.append((dst, src))
            for dst, src in split:
                sp.dma_start(dst, src).then_inc(att_params, 16)
            assert len(split) == PARAM_DMAS
            sp.dma_start(x_sb[:, TILES:, :], x_rows[:, TILES:, :]).then_inc(x_rest, 16)
            sp.dma_start(wi_gu[:, :, 0, :], rows(w_gate_t)).then_inc(weights_loaded, 16)
            sp.dma_start(wi_gu[:, :, 1, :], rows(w_up_t)).then_inc(weights_loaded, 16)
            sp.dma_start(wi_d[:], rows(w_down_t)).then_inc(weights_loaded, 16)

            def stack_q(n, parity):
                sp.wait_ge(q_hi_done, DT * n + DT)
                sp.wait_ge(q_lo_done, DT * n + DT)
                for block_row, part in ((0, q_hi), (32, q_hi), (64, q_lo)):
                    for j in range(4):
                        sp.dma_start(q_stack[block_row:block_row + 32, parity, j:PAIRS:4, :],
                                     part[32 * j:32 * j + 32, :, :]).then_inc(q_stacked, 16)

            def stack_max(n, parity):
                sp.wait_ge(mxt_sb, n + 1)
                for r in range(2):
                    sp.dma_start(q_stack[MAX_ROW + r:MAX_ROW + r + 1, parity, :, :],
                                 neg_max_t[r:HEADS:2, :]).then_inc(max_stacked, 16)

            def next_v(c, b, g):
                sp.wait_ge(pv_psum, GROUPS * c + (g + 1 + CREDIT["pv_psum"]))
                sp.dma_start(v_cur[0:ROWS, 2 * g:2 * g + 2, :, :, :],
                             v_all[0:ROWS, b + 1, 2 * g:2 * g + 2, :, :, :]).then_inc(v_ready[g], 16)

            sp.wait_ge(pool_init, 5)
            sp.wait_ge(k_split, DT)
            for block_row, part in ((0, k_hi), (32, k_lo), (64, k_hi)):
                for t in range(DT):
                    for j in range(4):
                        for r in range(2):
                            sp.dma_start(
                                k_stack[block_row + DH * r:block_row + DH * r + DH, :, 4 * t + j,
                                        r * KEYS:r * KEYS + KEYS],
                                part[32 * j + DH * r:32 * j + DH * r + DH, t, :, :]).then_inc(k_stacked, 16)
            sp.wait_ge(pool_init, 10)
            for parity in range(2):
                sp.dma_start(q_stack[MASK_ROW:MASK_ROW + 1, parity, :, :],
                             mask_ones[0:1, :].unsqueeze(1).broadcast_to([1, PAIRS, CHUNK])).then_inc(k_stacked, 16)
            sp.wait_ge(mask_step, 4)
            for b in range(BATCH):
                for r in range(2):
                    sp.dma_start(k_stack[MASK_ROW:MASK_ROW + 1, b, :, r * KEYS:r * KEYS + KEYS],
                                 mask_row[0:1, b, :].unsqueeze(1).broadcast_to([1, PAIRS, KEYS])).then_inc(k_stacked, 16)
                    sp.dma_start(k_stack[MAX_ROW + r:MAX_ROW + r + 1, b, :, r * KEYS:r * KEYS + KEYS],
                                 unit_row[0:1, :].unsqueeze(1).broadcast_to([1, PAIRS, KEYS])).then_inc(k_stacked, 16)
            stack_q(0, 0)
            sp.wait_ge(v_step, 2 + 4)
            sp.wait_ge(v_done, 2)
            for g in range(GROUPS):
                sp.dma_start(v_cur[0:ROWS, 2 * g:2 * g + 2, :, :, :],
                             v_all[0:ROWS, 0, 2 * g:2 * g + 2, :, :, :]).then_inc(v_ready[g], 16)
            stack_max(0, 0)

            def chunk(c, b, j, prepares, more_batches):
                if prepares:
                    stack_q(c + 1, 1 - j)
                if j == PER_BATCH - 1 and more_batches:
                    for g in range(GROUPS - 1):
                        next_v(c, b, g)
                if prepares:
                    stack_max(c + 1, 1 - j)
                if j == PER_BATCH - 1 and more_batches:
                    next_v(c, b, GROUPS - 1)

            all_chunks(sp, chunk)
            sp.wait_ge(weights_loaded, 48)

        @block.gpsimd
        def _(pool):
            pool.memset(ident[:], 0.0).then_inc(pool_init, 1)
            pool.memset(k_stack[:].rearrange("p b a k -> p (b a k)").bitcast(mybir.dt.uint32), 0).then_inc(pool_init, 1)
            pool.memset(head_rows[:], 1.0).then_inc(pool_init, 1)
            pool.memset(minus_half[:], -0.5).then_inc(pool_init, 1)
            pool.memset(eps[:], EPS).then_inc(pool_init, 1)
            pool.wait_ge(pool_init, 5)
            pool.affine_select(out=ident[:], in_=ident[:], compare_op=ALU.not_equal, fill=1.0, base=0,
                               pattern=[[-1, P]], channel_multiplier=1).then_inc(pool_init, 1)
            pool.affine_select(out=head_rows[:, 0:1], in_=head_rows[:, 0:1], compare_op=ALU.is_gt, fill=0.0,
                               base=SPLIT, pattern=[[0, 1]], channel_multiplier=-1).then_inc(pool_init, 1)
            pool.affine_select(out=head_rows[:, 1:2], in_=head_rows[:, 1:2], compare_op=ALU.is_ge, fill=0.0,
                               base=-SPLIT, pattern=[[0, 1]], channel_multiplier=1).then_inc(pool_init, 1)
            pool.memset(unit_row[:], MAX_UNIT).then_inc(pool_init, 1)
            pool.memset(mask_ones[:], MASK_ONE).then_inc(pool_init, 1)

            def prepare(n):
                inverse_deviation(pool, n, stats_done, pool_step, var_eps, mean_var, eps, minus_half, rstd)
                pool.wait_ge(normed, n + 1)
                pool.wait_ge(params_ready, 5)
                rows_n = x_sb[:, bass.ds(TILES * n, TILES), :]
                pool.tensor_tensor(rows_n, rows_n, bo[:].unsqueeze(1).broadcast_to([P, TILES, DIM]), ALU.add).then_inc(residual_ready, 1)

            prepare(0)
            prepare(1)
            with pool.Fori(0, CHUNKS - 2) as c:
                prepare(c + 2)

        @block.scalar
        def _(act):
            act.sem_inc(exp_done, CREDIT["exp_done"])
            act.sem_inc(pv_sb, CREDIT["pv_sb"])
            act.wait_ge(att_params, 16 * PARAM_DMAS)
            act.activation(att_gate[:], gates[:, 0:1], ACT.Tanh).then_inc(gates_tanh, 1)
            act.activation(ffn_gate[:], gates[:, 1:2], ACT.Tanh).then_inc(gates_tanh, 1)

            def xt_copy(n, t):
                act.wait_ge(xt_psum, DT * n + t + 1)
                if not first(n):
                    act.wait_ge(q_psum, DT * n)
                act.copy(xh_t[:, t, :], work[t][:, :]).then_inc(xt_sb, 1)

            def q_copy(n, t):
                act.wait_ge(q_psum, DT * n + t + 1)
                if not first(n):
                    act.wait_ge(q_stacked, 16 * STACK_DMAS * n)
                act.activation(q_hi[:, t, :], work[t][:, :], ACT.Identity, bias=bq[:, t:t + 1]).then_inc(q_hi_done, 1)

            def exp_tile(c, i):
                act.wait_ge(st_psum, ST_PER_CHUNK * c + i + 1)
                if i % ST_PER_GROUP == 0:
                    act.wait_ge(pv_psum, GROUPS * c + (i // ST_PER_GROUP - 1 + CREDIT["pv_psum"]))
                n = TILE_ROWS[i % 3]
                act.activation(probs[0:n, i % (2 * ST_PER_GROUP), :], st_bank[i % 2][0:n, :], ACT.Exp,
                               scale=EXP_SCALE).then_inc(exp_done, 1)

            def pv_copy(c, g):
                act.wait_ge(pv_psum, GROUPS * c + (g + 1 + CREDIT["pv_psum"]))
                act.wait_ge(nt_psum, GROUPS * c + (g - 1 + CREDIT["nt_psum"]))
                act.copy(ou[:, g % 2, :], pv_bank[g % 2][:, :]).then_inc(pv_sb, 1)

            def at_copy(c, t):
                act.wait_ge(at_psum, DT * c + (t + 1 + CREDIT["at_psum"]))
                act.wait_ge(o_psum, 2 * c + CREDIT["o_psum"])
                act.copy(att_t[:, t, :], work[0][:, :]).then_inc(at_sb, 1)

            act.mul(wq[:], wq[:], QK_SCALE).then_inc(params_ready, 1)
            act.mul(bq[:], bq[:], QK_SCALE).then_inc(params_ready, 1)
            act.wait_ge(params_ready, 5)
            for t in range(DT):
                xt_copy(0, t)
            for t in range(DT):
                q_copy(0, t)

            def chunk(c, b, j, prepares, more_batches):
                n = c + 1
                exp_tile(c, 0)
                if prepares:
                    xt_copy(n, 0)
                exp_tile(c, 1)
                if prepares:
                    xt_copy(n, 1)
                exp_tile(c, 2)
                if prepares:
                    q_copy(n, 0)
                exp_tile(c, 3)
                exp_tile(c, 4)
                if prepares:
                    q_copy(n, 1)
                exp_tile(c, 5)
                for g in range(1, GROUPS):
                    for i in range(ST_PER_GROUP):
                        exp_tile(c, ST_PER_GROUP * g + i)
                        if i == 3:
                            pv_copy(c, g - 1)
                    if g == 3:
                        at_copy(c, 0)
                pv_copy(c, GROUPS - 1)
                at_copy(c, 1)

            all_chunks(act, chunk)

        @block.vector
        def _(dve):
            dve.sem_inc(mx_reduced, CREDIT["mx_reduced"])
            dve.sem_inc(x1_done, CREDIT["x1_done"])

            def chunk_stats(n):
                row_stats(dve, n, x_sb, stats, mean_var, stats_step, stats_done, normed, waiter)

            def chunk_norm(n):
                normalise_rows(dve, n, x_sb, xh, mean_var, rstd, pool_step, xt_psum, normed)

            dve.wait_ge(x_first, 16)
            chunk_stats(0)
            chunk_norm(0)
            dve.wait_ge(att_params, 16 * PARAM_DMAS)
            dve.tensor_scalar(wk[:], wk[:], QK_SCALE, None, ALU.mult).then_inc(params_ready, 1)
            dve.tensor_scalar(bk[:], bk[:], QK_SCALE, None, ALU.mult).then_inc(params_ready, 1)
            dve.wait_ge(gates_tanh, 2)
            dve.tensor_scalar(wo[:], wo[:], att_gate[:, 0:1], None, ALU.mult).then_inc(v_step, 1)
            dve.tensor_scalar(bo[:], bo[:], att_gate[:, 0:1], None, ALU.mult).then_inc(params_ready, 1)
            dve.wait_ge(params_ready, 5)
            dve.tensor_copy(mask_f[:], mask_u8[:]).then_inc(mask_step, 1)
            dve.wait_ge(mask_step, 1)
            dve.tensor_reduce(some_valid[:], mask_f[:], AX.X, ALU.min).then_inc(mask_step, 1)
            dve.wait_ge(mask_step, 2)
            dve.tensor_scalar(some_valid[:], some_valid[:], -1.0, 1.0, ALU.mult, ALU.add).then_inc(mask_step, 1)
            dve.wait_ge(mask_step, 3)
            for b in range(BATCH):
                last = dve.tensor_scalar(mask_row[:, b, :], mask_f[:, b, :], some_valid[:, b:b + 1], -MASK_ONE,
                                         ALU.mult, ALU.mult)
            last.then_inc(mask_step, 1)
            for t in range(DT):
                for half in range(2):
                    dve.wait_ge(k_psum, 2 * t + half + 1)
                    for b in range(2):
                        last = dve.tensor_scalar(k_f[:, t, 2 * half + b, :],
                                                 st_bank[half][:, b * KEYS:b * KEYS + KEYS], bk[:, t:t + 1],
                                                 some_valid[:, 2 * half + b:2 * half + b + 1], ALU.add, ALU.mult)
                    last.then_inc(k_step, 1)
                dve.wait_ge(k_step, 3 * t + 2)
                dve.tensor_copy(k_hi[:, t], k_f[:, t]).then_inc(k_step, 1)
                dve.wait_ge(k_step, 3 * t + 3)
                dve.tensor_tensor(k_lo[:, t], k_f[:, t], k_hi[:, t], ALU.subtract).then_inc(k_split, 1)

            def q_low(n, t):
                dve.wait_ge(q_hi_done, DT * n + t + 1)
                if not first(n):
                    dve.wait_ge(q_stacked, 16 * STACK_DMAS * n)
                dve.scalar_tensor_tensor(q_lo[:, t, :], work[t][:, :], bq[:, t:t + 1], q_hi[:, t, :],
                                         ALU.add, ALU.subtract).then_inc(q_lo_done, 1)

            for t in range(DT):
                q_low(0, t)
            dve.wait_ge(x_rest, 16)
            chunk_stats(1)
            chunk_norm(1)

            dve.memset(v_all[:, :, :, :, 1, :], 1.0)
            dve.memset(v_all[96:P, :, :, 3, 0, :], 0.0).then_inc(v_step, 1)
            dve.wait_ge(v_step, 2)
            dve.wait_ge(pool_init, 10)
            bv_heads = bv[:].rearrange("p (a r d) -> p a r d", r=2, d=DH)
            for b in range(BATCH):
                for part, (tile, r) in enumerate(PV_PARTS):
                    m = TILE_ROWS[tile]
                    if part != 2:
                        dve.wait_ge(v_psum, 3 * b + tile + 1)
                    src = st_bank[tile % 2] if tile < 2 else pv_bank[0]
                    heads = src[0:m, 0:DIM].rearrange("p (a r d) -> p a r d", r=2, d=DH)[:, :, r, :]
                    dve.tensor_tensor(v_all[0:m, b, :, part, 0, :], heads, bv_heads[0:m, :, r, :],
                                      ALU.add).then_inc(v_step, 1)
                    if tile == 1:
                        dve.wait_ge(v_step, 4 * b + part + 3)
                        both = v_all[0:m, b, :, part, :, :]
                        dve.tensor_scalar(both, both, head_rows[0:m, r:r + 1], None, ALU.mult).then_inc(v_done, 1)

            def max_tile(n, t, p):
                m = PAIRS * t + p
                if m == 0:
                    if not first(n):
                        dve.wait_ge(mxt_psum, n)
                dve.wait_ge(mx_psum, MX * n + m + 1)
                dve.tensor_reduce(neg_max[:, t, 2 * p:2 * p + 2],
                                  mx_bank[m % 2][:, 0:PAIR_KEYS].rearrange("q (r k) -> q r k", r=2),
                                  AX.X, ALU.max, negate=True).then_inc(mx_reduced, 1)

            def max_copy(n):
                dve.wait_ge(mxt_psum, n + 1)
                if not first(n):
                    dve.wait_ge(max_stacked, 16 * 2 * n)
                dve.tensor_scalar(neg_max_t[:, :], work[0][0:HEADS, :], 1.0 / MAX_UNIT, None,
                                  ALU.mult).then_inc(mxt_sb, 1)

            def normalise(c, g, bank_of):
                src = bank_of[:, :].rearrange("q (t h e d) -> q t h e d", t=TILES, h=4, e=2)
                dve.wait_ge(nt_psum, GROUPS * c + (g + 1 + CREDIT["nt_psum"]))
                dve.reciprocal(rec[:, g % 2], src[:, :, :, 1, 0]).then_inc(rec_done, 1)
                dve.wait_ge(rec_done, GROUPS * c + g + 1)
                dve.wait_ge(at_psum, DT * c + CREDIT["at_psum"])
                dst = att[:, :, 4 * DH * g:4 * DH * (g + 1)].rearrange("q t (h d) -> q t h d", h=4)
                dve.tensor_tensor(dst, src[:, :, :, 0, :], rec[:, g % 2].unsqueeze(3).broadcast_to([P, TILES, 4, DH]),
                                  ALU.mult).then_inc(att_done, 1)

            def residual(c, u):
                dve.wait_ge(o_psum, 2 * c + (u + 1 + CREDIT["o_psum"]))
                dve.wait_ge(residual_ready, c + 1)
                rows = x_sb[:, bass.ds(TILES * c + 2 * u, 2), :]
                dve.tensor_tensor(rows, rows, work[1 - u][:, :].rearrange("q (t d) -> q t d", t=2),
                                  ALU.add).then_inc(x1_done, 1)

            for t in range(TILES):
                for p in range(PAIRS):
                    max_tile(0, t, p)
            max_copy(0)

            def chunk(c, b, j, prepares, more_batches):
                n = c + 1
                if prepares:
                    for t in range(DT):
                        q_low(n, t)
                if more_batches:
                    chunk_stats(c + 2)
                    chunk_norm(c + 2)
                for g in range(1, GROUPS):
                    if prepares:
                        for p in range(PAIRS):
                            max_tile(n, g - 1, p)
                    if g >= 2:
                        normalise(c, g - 2, work[(g - 2) % 2])
                normalise(c, 2, work[1])
                if prepares:
                    for p in range(PAIRS):
                        max_tile(n, TILES - 1, p)
                    max_copy(n)
                normalise(c, 3, work[1])
                for u in range(2):
                    residual(c, u)

            all_chunks(dve, chunk)

        @block.tensor
        def _(pe):
            pe.sem_inc(pv_psum, CREDIT["pv_psum"])
            pe.sem_inc(nt_psum, CREDIT["nt_psum"])
            pe.sem_inc(at_psum, CREDIT["at_psum"])
            pe.sem_inc(o_psum, CREDIT["o_psum"])

            def x_transposes(n, t):
                if t == 0:
                    pe.wait_ge(normed, n + 1)
                if isinstance(n, int) and n == 0:
                    pass
                else:
                    pe.wait_ge(x1_done, 2 * n + ((2 if t == 0 else 1) - 4 + CREDIT["x1_done"]))
                for i in range(TILES):
                    last = pe.transpose(work[t][:, P * i:P * i + P], xh[:, i, P * t:P * t + P], ident[:])
                last.then_inc(xt_psum, 1)

            def q_project(n, t):
                pe.wait_ge(xt_sb, DT * n + DT)
                for k in range(DT):
                    last = pe.matmul(work[t][:, :], wq[:, k, P * t:P * t + P], xh_t[:, k, :],
                                     start=(k == 0), stop=(k == DT - 1))
                last.then_inc(q_psum, 1)

            def max_scores(n, b, parity, t, p):
                m = PAIRS * t + p
                if m == 0:
                    pe.wait_ge(q_stacked, 16 * STACK_DMAS * (n + 1))
                pe.wait_ge(mx_reduced, MX * n + (m - 1 + CREDIT["mx_reduced"]))
                pe.matmul(mx_bank[m % 2][:, 0:PAIR_KEYS], q_stack[0:MAX_ROW, parity, p, P * t:P * t + P],
                          k_stack[0:MAX_ROW, b, p, :], start=True, stop=True).then_inc(mx_psum, 1)

            def max_transposes(n):
                pe.wait_ge(mx_reduced, MX * n + MX + CREDIT["mx_reduced"])
                for i in range(TILES):
                    last = pe.transpose(work[0][0:HEADS, P * i:P * i + P], neg_max[:, i, :], ident[:])
                last.then_inc(mxt_psum, 1)

            def scores(c, b, parity, i):
                if i == 0:
                    pe.wait_ge(max_stacked, 16 * 2 * (c + 1))
                g, tile = i // ST_PER_GROUP, i % 3
                p = i // 3
                m = TILE_ROWS[tile]
                pe.wait_ge(exp_done, ST_PER_CHUNK * c + (i - 1 + CREDIT["exp_done"]))
                pe.matmul(st_bank[i % 2][0:m, :], k_stack[0:STACK_ROWS, b, p, ROWS * tile:ROWS * tile + m],
                          q_stack[0:STACK_ROWS, parity, p, :], start=True, stop=True).then_inc(st_psum, 1)

            def values(c, b, g, second):
                if not second:
                    pe.wait_ge(exp_done, ST_PER_CHUNK * c + (ST_PER_GROUP * (g + 1) + CREDIT["exp_done"]))
                    pe.wait_ge(v_ready[g], 16 * b + 16)
                    pe.wait_ge(pv_sb, GROUPS * c + (g - 1 + CREDIT["pv_sb"]))
                for p in range(2):
                    for part in (2 * second, 2 * second + 1):
                        tile, r = PV_PARTS[part]
                        m = TILE_ROWS[tile]
                        at = 32 * (2 * p + r)
                        last = pe.matmul(
                            pv_bank[g % 2][at:at + 32, :],
                            v_cur[0:m, 2 * g + p, part, :, :].rearrange("k e d -> k (e d)"),
                            probs[0:m, (ST_PER_GROUP * g + 3 * p + tile) % (2 * ST_PER_GROUP), :],
                            start=not second, stop=bool(second))
                if second:
                    last.then_inc(pv_psum, 1)

            def norm_transposes(c, g, bank_of):
                pe.wait_ge(pv_sb, GROUPS * c + (g + 1 + CREDIT["pv_sb"]))
                for i in range(TILES):
                    last = pe.transpose(bank_of[:, P * i:P * i + P], ou[:, g % 2, P * i:P * i + P], ident[:])
                last.then_inc(nt_psum, 1)

            def att_transposes(c, t):
                pe.wait_ge(att_done, GROUPS * c + 2 * t + 2)
                for i in range(TILES):
                    last = pe.transpose(work[0][:, P * i:P * i + P], att[:, i, P * t:P * t + P], ident[:])
                last.then_inc(at_psum, 1)

            def out_project(c, u):
                if u == 0:
                    pe.wait_ge(at_sb, DT * c + DT)
                for i in range(2):
                    for k in range(DT):
                        q0 = P * (2 * u + i)
                        last = pe.matmul(work[1 - u][:, DIM * i:DIM * i + DIM], att_t[:, k, q0:q0 + P],
                                         wo[:, k, :], start=(k == 0), stop=(k == DT - 1))
                last.then_inc(o_psum, 1)

            pe.wait_ge(att_params, 16 * PARAM_DMAS)
            pe.wait_ge(params_ready, 5)
            pe.wait_ge(pool_init, 10)
            for t in range(DT):
                for half in range(2):
                    if t:
                        pe.wait_ge(k_step, half + 1)
                    for k in range(DT):
                        last = pe.matmul(st_bank[half][:, 0:PAIR_KEYS], wk[:, k, P * t:P * t + P],
                                         ctx2[:, k, 2 * half:2 * half + 2, 0, :], start=(k == 0), stop=(k == DT - 1))
                    last.then_inc(k_psum, 1)
            for t in range(DT):
                x_transposes(0, t)
            for t in range(DT):
                q_project(0, t)
            pe.wait_ge(k_split, DT)
            for b in range(BATCH):
                for tile in range(3):
                    m = TILE_ROWS[tile]
                    dst = st_bank[tile % 2] if tile < 2 else pv_bank[0]
                    if b:
                        pe.wait_ge(v_step, 2 + 4 * (b - 1) + (1, 3, 4)[tile])
                    keys = ctx2[:, :, b, :, :].rearrange("p t r k -> p t (r k)")
                    for k in range(DT):
                        last = pe.matmul(dst[0:m, 0:DIM], keys[:, k, ROWS * tile:ROWS * tile + m], wv[:, k, :],
                                         start=(k == 0), stop=(k == DT - 1))
                    last.then_inc(v_psum, 1)
            pe.wait_ge(k_stacked, 16 * K_STACK_DMAS)
            for t in range(TILES):
                for p in range(PAIRS):
                    max_scores(0, 0, 0, t, p)
            pe.wait_ge(q_lo_done, 1)
            max_transposes(0)
            pe.wait_ge(mxt_sb, 1)
            pe.wait_ge(q_lo_done, DT)
            pe.wait_ge(v_step, 2 + 4 * BATCH)

            def chunk(c, b, j, prepares, more_batches):
                n, nb, nj = c + 1, (b if j == 0 else b + 1), 1 - j

                def maxes(t, first, last):
                    if prepares:
                        for p in range(first, last):
                            max_scores(n, nb, nj, t, p)

                scores(c, b, j, 0)
                if prepares:
                    x_transposes(n, 0)
                scores(c, b, j, 1)
                if prepares:
                    x_transposes(n, 1)
                scores(c, b, j, 2)
                if prepares:
                    q_project(n, 0)
                scores(c, b, j, 3)
                scores(c, b, j, 4)
                if prepares:
                    q_project(n, 1)
                scores(c, b, j, 5)
                for g in range(1, GROUPS):
                    i = ST_PER_GROUP * g
                    for s in range(2):
                        scores(c, b, j, i + 2 * s)
                        maxes(g - 1, 2 * s, 2 * s + 1)
                        scores(c, b, j, i + 2 * s + 1)
                        maxes(g - 1, 2 * s + 1, 2 * s + 2)
                        values(c, b, g - 1, s)
                    scores(c, b, j, i + 4)
                    maxes(g - 1, 4, 5)
                    scores(c, b, j, i + 5)
                    maxes(g - 1, 5, PAIRS)
                    if g == 2:
                        if prepares:
                            pe.wait_ge(q_lo_done, DT * n + 1)
                        else:
                            pe.wait_ge(x1_done, 2 * c + CREDIT["x1_done"])
                        norm_transposes(c, 0, work[0])
                    if g == 3:
                        if prepares:
                            pe.wait_ge(q_lo_done, DT * n + 2)
                        norm_transposes(c, 1, work[1])
                        att_transposes(c, 0)
                pe.wait_ge(att_done, GROUPS * c + 2)
                norm_transposes(c, 2, work[1])
                maxes(TILES - 1, 0, PAIRS)
                values(c, b, GROUPS - 1, 0)
                values(c, b, GROUPS - 1, 1)
                if prepares:
                    pe.wait_ge(at_sb, DT * c + 1)
                    max_transposes(n)
                pe.wait_ge(att_done, GROUPS * c + 3)
                norm_transposes(c, 3, work[1])
                if prepares:
                    pe.wait_ge(mxt_sb, n + 1)
                else:
                    pe.wait_ge(at_sb, DT * c + 1)
                att_transposes(c, 1)
                out_project(c, 0)
                out_project(c, 1)

            all_chunks(pe, chunk)


PARAM_DMAS = 15
K_STACK_DMAS = 3 * DT * 4 * 2 + 2 + 4 * BATCH


def feed_forward(nc, st, sb, sem, out_rows, x_sb, ident, ffn_gate, wi_gu, wi_d, stats, mean_var,
                 var_eps, eps, minus_half, rstd, xh, xh_t, weights_loaded):
    def f_sb(name, shape, dtype=F32):
        return sb(name, shape, dtype, st)

    def f_sem(name):
        return sem(name, st)

    w_gu = f_sb("w_gu", [P, DT, 2, HIDDEN])
    w_d = f_sb("w_d", [P, HT, DIM])
    waiter = f_sb("f_waiter", [P, 1])
    silu = f_sb("silu", [P, 2, CHUNK])
    hidden = f_sb("hidden", [P, 2, HT, CHUNK])
    out_gate = f_sb("out_gate", [P, 1])

    def bank(name):
        return st.enter_context(nc.psum_tensor(name, [P, 512], F32))

    xt_bank = [bank(f"xt_bank{i}") for i in range(2)]
    gate_bank = [bank(f"gate_bank{i}") for i in range(2)]
    up_bank = [bank(f"up_bank{i}") for i in range(2)]
    down_bank = [bank(f"down_bank{i}") for i in range(2)]

    w_ready = f_sem("w_ready")
    stats_step = f_sem("f_stats_step")
    stats_done = f_sem("f_stats_done")
    pool_step = f_sem("f_pool_step")
    normed = f_sem("f_normed")
    xt_psum = f_sem("f_xt_psum")
    xt_sb = f_sem("f_xt_sb")
    gate_psum = f_sem("gate_psum")
    up_psum = f_sem("up_psum")
    silu_done = f_sem("silu_done")
    hidden_done = f_sem("hidden_done")
    down_psum = f_sem("down_psum")
    y_done = f_sem("y_done")
    stored = f_sem("stored")

    Y_CREDIT = 2

    def loop(engine, chunk):
        chunk(0, 0)
        with engine.Fori(0, (CHUNKS - 2) // 2) as i:
            for j in range(2):
                chunk(2 * i + 1 + j, 1 - j)
        chunk(CHUNKS - 1, (CHUNKS - 1) % 2)

    with nc.Block() as block:

        @block.sync
        def _(sp):
            def chunk(c, parity):
                sp.wait_ge(y_done, 2 * c + (2 + Y_CREDIT))
                rows = bass.ds(TILES * c, TILES)
                sp.dma_start(out_rows[:, rows, :], x_sb[:, rows, :]).then_inc(stored, 16)
            loop(sp, chunk)
            sp.wait_ge(stored, 16 * CHUNKS)

        @block.gpsimd
        def _(pool):
            def chunk(n, parity):
                inverse_deviation(pool, n, stats_done, pool_step, var_eps, mean_var, eps, minus_half, rstd)
            loop(pool, chunk)

        @block.scalar
        def _(act):
            act.activation(w_gu[:], wi_gu[:], ACT.Copy, scale=WEIGHT_SCALE).then_inc(w_ready, 1)

            def chunk(c, parity):
                for t in range(DT):
                    act.wait_ge(xt_psum, DT * c + t + 1)
                    if not first(c) and t == 0:
                        act.wait_ge(up_psum, HT * c)
                    act.copy(xh_t[:, t, :], xt_bank[t][:, :]).then_inc(xt_sb, 1)
                for h in range(HT):
                    act.wait_ge(gate_psum, HT * c + h + 1)
                    if not (first(c) and h < 2):
                        act.wait_ge(hidden_done, HT * c + h - 1)
                    act.activation(silu[:, h % 2, :], gate_bank[h % 2][:, :], ACT.Silu).then_inc(silu_done, 1)
            loop(act, chunk)

        @block.vector
        def _(dve):
            dve.sem_inc(y_done, Y_CREDIT)
            dve.tensor_scalar(w_d[:], wi_d[:], WEIGHT_SCALE, None, ALU.mult).then_inc(w_ready, 1)

            def chunk_stats(n):
                row_stats(dve, n, x_sb, stats, mean_var, stats_step, stats_done, normed, waiter)

            def chunk_norm(n):
                normalise_rows(dve, n, x_sb, xh, mean_var, rstd, pool_step, xt_psum, normed)

            chunk_stats(0)
            chunk_norm(0)

            def residual(c, u):
                dve.wait_ge(down_psum, 2 * c + u + 1)
                rows = x_sb[:, bass.ds(TILES * c + 2 * u, 2), :]
                dve.scalar_tensor_tensor(rows, down_bank[u][:, :].rearrange("q (t d) -> q t d", t=2),
                                         ffn_gate[:, 0:1], rows, ALU.mult, ALU.add).then_inc(y_done, 1)

            def chunk(c, parity):
                last_chunk = isinstance(c, int) and c == CHUNKS - 1
                if not last_chunk:
                    chunk_stats(c + 1)
                    chunk_norm(c + 1)
                for h in range(HT):
                    dve.wait_ge(up_psum, HT * c + h + 1)
                    dve.wait_ge(silu_done, HT * c + h + 1)
                    dve.tensor_tensor(hidden[:, parity, h, :], up_bank[h % 2][:, :], silu[:, h % 2, :],
                                      ALU.mult).then_inc(hidden_done, 1)
                    if h == 2 and not first(c):
                        for u in range(2):
                            residual(c - 1, u)
                if last_chunk:
                    for u in range(2):
                        residual(c, u)
            loop(dve, chunk)

        @block.tensor
        def _(pe):
            pe.wait_ge(w_ready, 2)

            def x_transposes(n):
                pe.wait_ge(normed, n + 1)
                for t in range(DT):
                    if not first(n):
                        pe.wait_ge(xt_sb, DT * n)
                    for i in range(TILES):
                        last = pe.transpose(xt_bank[t][:, P * i:P * i + P], xh[:, i, P * t:P * t + P], ident[:])
                    last.then_inc(xt_psum, 1)

            def gate_up(c, h):
                if not (first(c) and h < 2):
                    pe.wait_ge(hidden_done, HT * c + h - 1)
                for which, (banks, done) in enumerate(((gate_bank, gate_psum), (up_bank, up_psum))):
                    for k in range(DT):
                        last = pe.matmul(banks[h % 2][:, :], w_gu[:, k, which, P * h:P * h + P], xh_t[:, k, :],
                                         start=(k == 0), stop=(k == DT - 1))
                    last.then_inc(done, 1)

            def down(c, parity, u):
                pe.wait_ge(hidden_done, HT * c + HT)
                pe.wait_ge(y_done, 2 * c + (u - 1 + Y_CREDIT))
                for i in range(2):
                    q0 = P * (2 * u + i)
                    for h in range(HT):
                        last = pe.matmul(down_bank[u][:, DIM * i:DIM * i + DIM], hidden[:, parity, h, q0:q0 + P],
                                         w_d[:, h, :], start=(h == 0), stop=(h == HT - 1))
                last.then_inc(down_psum, 1)

            x_transposes(0)

            def chunk(c, parity):
                pe.wait_ge(xt_sb, DT * c + DT)
                for h in range(HT):
                    gate_up(c, h)
                    if h == 1 and not first(c):
                        for u in range(2):
                            down(c - 1, 1 - parity, u)
                if isinstance(c, int) and c == CHUNKS - 1:
                    for u in range(2):
                        down(c, parity, u)
                else:
                    x_transposes(c + 1)
            loop(pe, chunk)


def kernel(**inputs):
    import numpy as _np
    import concourse.bacc as _bacc
    from concourse import mybir as _mybir
    from concourse.bass_utils import run_bass_kernel_spmd as _run

    a = {k: _np.asarray(v) for k, v in inputs.items()}
    ctx = a["ctx_1024"]
    laid_out = {
        "x": a["x"],
        "ctx_t": ctx.reshape(-1, ctx.shape[-1]).T,
        "mask": a["mask_BxS2_bk0"],
        "g_xattn": a["g_xattn"],
        "g_ffn": a["g_ffn"],
        "w_q": a["L0_xattn_W_Q"], "b_q": a["L0_xattn_b_Q"].reshape(DT, P).T,
        "w_k": a["L0_xattn_W_K"], "b_k": a["L0_xattn_b_K"].reshape(DT, P).T,
        "w_v": a["L0_xattn_W_V"], "b_v": a["L0_xattn_b_V"],
        "w_o": a["L0_xattn_W_O"], "b_o": a["L0_xattn_b_O"],
        "w_gate_t": a["L0_ffn_w_gate"].T,
        "w_up_t": a["L0_ffn_w_up"].T,
        "w_down_t": a["L0_ffn_w_down"].T,
    }
    nc = _bacc.Bacc("TRN2", target_bir_lowering=False, num_devices=1)
    arrays, args = {}, []
    for name, value in laid_out.items():
        value = _np.ascontiguousarray(value)
        arrays[f"in_{name}_dram"] = value
        args.append(nc.dram_tensor(f"in_{name}_dram", value.shape, _mybir.dt.from_np(value.dtype), kind="ExternalInput").ap())
    out = nc.dram_tensor("out_0_dram", a["x"].shape, _mybir.dt.float32, kind="ExternalOutput").ap()
    flamingo_block(nc, *args, out)
    r = _run(nc, [arrays], core_ids=[0])
    return r.results[0]["out_0_dram"]
```

```python
from contextlib import ExitStack

import concourse.bass as bass
from concourse import mybir

ALU = mybir.AluOpType
ACT = mybir.ActivationFunctionType
AX = mybir.AxisListType
F32 = mybir.dt.float32
F16 = mybir.dt.float16
I32 = mybir.dt.int32
U8 = mybir.dt.uint8

P = 128
EPS = 1e-5
WEIGHT_SCALE = 1.0 / 127.0

BATCH, SEQ, DIM = 4, 1024, 256
KEYS = 154
HEADS = 16
DH = DIM // HEADS
HIDDEN = 768

CHUNK = 512
TILES = CHUNK // P
CHUNKS = BATCH * SEQ // CHUNK
PER_BATCH = SEQ // CHUNK
DT = DIM // P
HT = HIDDEN // P
PAIRS = HEADS // 2
GROUPS = PAIRS // 2
PAIR_KEYS = 2 * KEYS
HALF_PAIRS = PAIRS // DT
ROWS = 103
TILE_ROWS = [ROWS, ROWS, PAIR_KEYS - 2 * ROWS]
SPLIT = KEYS - ROWS
ST_PER_GROUP = 2 * len(TILE_ROWS)
ST_PER_CHUNK = GROUPS * ST_PER_GROUP
PV_PARTS = [(0, 0), (1, 1), (1, 0), (2, 1)]

QK_SCALE = 16.0
MASK_ROW = 3 * 32
MAX_ROW = P - 2
MASK_ONE = 32768.0
MAX_UNIT = 4096.0
EXP_SCALE = 1.0 / (QK_SCALE * QK_SCALE * DH ** 0.5)

NARROW_MAX = 127.0
X_SCALE = 1024.0
HIDDEN_SCALE = 0.25

STACK_DMAS = 3


K_STACK_DMAS = 3 * 2 + BATCH + 3


def flamingo_block(nc, x, ctx_t, mask, g_xattn, g_ffn, w_q, b_q, w_k, b_k, w_v, b_v, w_o, b_o,
                   w_gate_t, w_up_t, w_down_t, out):
    x_rows = x.rearrange("b (n p) d -> p (b n) d", p=P)
    out_rows = out.rearrange("b (n p) d -> p (b n) d", p=P)

    with ExitStack() as ctx:
        def sb(name, shape, dtype=F32, stack=ctx):
            return stack.enter_context(nc.sbuf_tensor(name, shape, dtype))

        def sem(name, stack=ctx):
            return stack.enter_context(nc.semaphore(name))

        x_sb = sb("x_sb", [P, CHUNKS * TILES, DIM])
        ident = sb("ident", [P, P])
        ffn_gate = sb("ffn_gate", [P, 1])
        wi_gu = sb("wi_gu", [P, DT, 2, HIDDEN], I32)
        wi_d = sb("wi_d", [P, HT, DIM], I32)
        stats = sb("stats", [P, TILES, 6])
        mean_var = sb("mean_var", [P, TILES, 2])
        var_eps = sb("var_eps", [P, TILES])
        minus_half = sb("minus_half", [P, TILES])
        eps = sb("eps", [P, TILES])
        rstd = sb("rstd", [P, TILES])
        xh = sb("xh", [P, TILES, DIM])
        xh_t = sb("xh_t", [P, DT, CHUNK])
        weights_loaded = sem("weights_loaded")
        w_gu16 = sb("w_gu16", [P, DT, 2, HIDDEN], F16)
        w_d16 = sb("w_d16", [P, HT, DIM], F16)
        narrow_flag = sb("narrow_flag", [1, 1], I32)

        with ExitStack() as att_stack:
            attention(nc, att_stack, sb, sem, x_rows, x_sb, ident, ffn_gate, wi_gu, wi_d, stats,
                      mean_var, var_eps, eps, minus_half, rstd, xh, xh_t, weights_loaded,
                      w_gu16, w_d16, narrow_flag, ctx_t, mask, g_xattn, g_ffn, w_q, b_q, w_k, b_k, w_v, b_v, w_o, b_o,
                      w_gate_t, w_up_t, w_down_t)
        narrow = nc.values_load(narrow_flag[0:1, 0:1], min_val=0, max_val=1)
        with nc.If(narrow != 0):
            with ExitStack() as ffn_stack:
                feed_forward_narrow(nc, ffn_stack, sb, sem, out_rows, x_sb, ident, ffn_gate, w_gu16, w_d16,
                                    stats, mean_var, var_eps, eps, minus_half, rstd, xh)
        with nc.Else():
            with ExitStack() as ffn_stack:
                feed_forward(nc, ffn_stack, sb, sem, out_rows, x_sb, ident, ffn_gate, wi_gu, wi_d, stats,
                             mean_var, var_eps, eps, minus_half, rstd, xh, xh_t)


def first(n):
    return isinstance(n, int) and n == 0


def inverse_deviation(pool, n, stats_done, pool_step, var_eps, mean_var, eps, minus_half, rstd):
    pool.wait_ge(stats_done, n + 1)
    pool.tensor_tensor(var_eps[:], mean_var[:, :, 1], eps[:], ALU.add).then_inc(pool_step, 1)
    pool.wait_ge(pool_step, 2 * n + 1)
    pool.tensor_tensor(rstd[:], var_eps[:], minus_half[:], ALU.pow).then_inc(pool_step, 1)


def row_stats(dve, n, x_sb, stats, mean_var, stats_step, stats_done, normed, waiter):
    if not first(n):
        dve.wait_ge(normed, n)
    for t in range(TILES):
        last = dve.bn_stats(stats[:, t, :], x_sb[:, (TILES * n + t) % (TILES * CHUNKS), :])
    last.then_inc(stats_step, 1)
    dve.wait_ge(stats_step, n + 1)
    dve.tensor_copy(waiter[:], stats[:, 0, 0:1])
    for t in range(TILES):
        last = dve.bn_aggr(mean_var[:, t, :], stats[:, t, :])
    last.then_inc(stats_done, 1)


def normalise_rows(dve, n, x_sb, xh, mean_var, rstd, pool_step, xt_psum, normed):
    dve.wait_ge(pool_step, 2 * n + 2)
    if not first(n):
        dve.wait_ge(xt_psum, DT * n)
    for t in range(TILES):
        last = dve.tensor_scalar(xh[:, t, :], x_sb[:, TILES * n + t, :], mean_var[:, t, 0:1],
                                 rstd[:, t:t + 1], ALU.subtract, ALU.mult)
    last.then_inc(normed, 1)


def attention(nc, st, sb, sem, x_rows, x_sb, ident, ffn_gate, wi_gu, wi_d, stats, mean_var, var_eps,
              eps, minus_half, rstd, xh, xh_t, weights_loaded, w_gu16, w_d16, narrow_flag, ctx_t, mask, g_xattn, g_ffn,
              w_q, b_q, w_k, b_k, w_v, b_v, w_o, b_o, w_gate_t, w_up_t, w_down_t):
    def a_sb(name, shape, dtype=F32):
        return sb(name, shape, dtype, st)

    def a_sem(name):
        return sem(name, st)

    wq = a_sb("wq", [P, DT, DIM])
    wk = a_sb("wk", [P, DT, DIM])
    wv = a_sb("wv", [P, DT, DIM])
    wo = a_sb("wo", [P, DT, DIM])
    bq = a_sb("bq", [P, DT])
    bk = a_sb("bk", [P, DT])
    bv = a_sb("bv", [P, DIM])
    bo = a_sb("bo", [P, DIM])
    gates = a_sb("gates", [P, 2])
    att_gate = a_sb("att_gate", [P, 1])
    ctx2 = a_sb("ctx2", [P, DT, BATCH, 2, KEYS])
    mask_u8 = a_sb("mask_u8", [P, BATCH, KEYS], U8)
    mask_f = a_sb("mask_f", [P, BATCH, KEYS])
    some_valid = a_sb("some_valid", [P, BATCH])
    mask_row = a_sb("mask_row", [P, BATCH, KEYS], F16)
    mask_ones = a_sb("mask_ones", [P, CHUNK], F16)
    unit_row = a_sb("unit_row", [P, KEYS], F16)
    q_scratch = nc.dram_tensor("q_scratch", (2, 2, DIM, CHUNK), F16).ap()
    k_scratch = nc.dram_tensor("k_scratch", (2, DIM, BATCH * KEYS), F16).ap()
    k_f = a_sb("k_f", [P, DT, BATCH, KEYS])
    k_hi = a_sb("k_hi", [P, DT, BATCH, KEYS], F16)
    k_lo = a_sb("k_lo", [P, DT, BATCH, KEYS], F16)
    k_stack = a_sb("k_stack", [P, BATCH, PAIRS, PAIR_KEYS], F16)
    v_all = a_sb("v_all", [P, BATCH, PAIRS, 4, 2, DH])
    v_cur = a_sb("v_cur", [P, PAIRS, 4, 2, DH])
    v_mid = a_sb("v_mid", [P, DIM])
    head_rows = a_sb("head_rows", [P, 2])
    q_hi = a_sb("q_hi", [P, DT, CHUNK], F16)
    q_lo = a_sb("q_lo", [P, DT, CHUNK], F16)
    q_stack = a_sb("q_stack", [P, 2, PAIRS, CHUNK], F16)
    waiter = a_sb("waiter", [P, 1])
    neg_max = a_sb("neg_max", [P, TILES, HEADS])
    neg_max_t = a_sb("neg_max_t", [HEADS, CHUNK], F16)
    w_top = a_sb("w_top", [P, 2])
    w_wide = a_sb("w_wide", [P, 2])
    ones_col = a_sb("ones_col", [P, 1])
    w_count = a_sb("w_count", [1, 1])
    probs = a_sb("probs", [P, 2 * ST_PER_GROUP, CHUNK])
    ou = a_sb("ou", [P, 2, CHUNK])
    rec = a_sb("rec", [P, 2, TILES, 4])
    att = a_sb("att", [P, TILES, DIM])
    att_t = a_sb("att_t", [P, DT, CHUNK])

    def bank(name):
        return st.enter_context(nc.psum_tensor(name, [P, 512], F32))

    work = [bank(f"work{i}") for i in range(2)]
    mx_bank = [bank(f"mx_bank{i}") for i in range(3)]
    st_bank = [bank(f"st_bank{i}") for i in range(2)]
    pv_bank = bank("pv_bank")

    k_params = a_sem("k_params")
    q_params = a_sem("q_params")
    v_params = a_sem("v_params")
    o_params = a_sem("o_params")
    mask_loaded = a_sem("mask_loaded")
    gate_params = a_sem("gate_params")
    bv_loaded = a_sem("bv_loaded")
    x_first = a_sem("x_first")
    x_second = a_sem("x_second")
    x_rest = a_sem("x_rest")
    pool_init = a_sem("pool_init")
    zeroed = a_sem("zeroed")
    params_ready = a_sem("params_ready")
    wo_ready = a_sem("wo_ready")
    bo_ready = a_sem("bo_ready")
    gates_tanh = a_sem("gates_tanh")
    mask_step = a_sem("mask_step")
    k_psum = a_sem("k_psum")
    k_step = a_sem("k_step")
    k_split = a_sem("k_split")
    v_psum = a_sem("v_psum")
    v_step = a_sem("v_step")
    v_done = a_sem("v_done")
    k_bounced = a_sem("k_bounced")
    k_stacked = a_sem("k_stacked")
    stats_done = a_sem("stats_done")
    stats_step = a_sem("stats_step")
    pool_step = a_sem("pool_step")
    centred = a_sem("centred")
    normed = a_sem("normed")
    residual_ready = a_sem("residual_ready")
    xt_psum = a_sem("xt_psum")
    xt_sb = a_sem("xt_sb")
    q_psum = a_sem("q_psum")
    q_hi_done = a_sem("q_hi_done")
    q_lo_done = a_sem("q_lo_done")
    q_hi_bounced = [a_sem(f"q_hi_bounced{t}") for t in range(DT)]
    q_lo_bounced = [a_sem(f"q_lo_bounced{t}") for t in range(DT)]
    q_stacked = [a_sem(f"q_stacked{t}") for t in range(DT)]
    mx_psum = a_sem("mx_psum")
    mx_reduced = a_sem("mx_reduced")
    mxt_psum = a_sem("mxt_psum")
    mxt_sb = a_sem("mxt_sb")
    max_stacked = a_sem("max_stacked")
    w_converted = a_sem("w_converted")
    wide_found = a_sem("wide_found")
    wide_counted = a_sem("wide_counted")
    narrow_set = a_sem("narrow_set")
    st_psum = a_sem("st_psum")
    exp_done = a_sem("exp_done")
    v_ready = [a_sem(f"v_ready{g}") for g in range(GROUPS)]
    pv_psum = a_sem("pv_psum")
    pv_sb = a_sem("pv_sb")
    nt_psum = a_sem("nt_psum")
    rec_done = a_sem("rec_done")
    att_done = a_sem("att_done")
    at_psum = a_sem("at_psum")
    at_sb = a_sem("at_sb")
    o_psum = a_sem("o_psum")
    x1_done = a_sem("x1_done")

    nt_bank = [work[0], work[1], work[0], mx_bank[1]]
    v_banks = [st_bank[0], st_bank[1], pv_bank]
    MX = TILES * PAIRS
    MX_STEPS = [0, 10, 21, MX]
    CREDIT = {"mx_reduced": 3, "exp_done": 2, "pv_psum": 2, "pv_sb": 2, "nt_psum": 2, "at_psum": DT,
              "o_psum": 2, "x1_done": 2}

    def all_chunks(engine, chunk):
        with engine.Fori(0, BATCH - 1) as b:
            for j in range(PER_BATCH):
                chunk(b * PER_BATCH + j, b, j)
        for j in range(PER_BATCH):
            chunk((BATCH - 1) * PER_BATCH + j, BATCH - 1, j)

    def max_place(m):
        half, rest = divmod(m, TILES * HALF_PAIRS)
        t, p = divmod(rest, HALF_PAIRS)
        return t, half * HALF_PAIRS + p

    def peeled(b):
        return isinstance(b, int)

    with nc.Block() as block:

        @block.sync
        def _(sp):
            rows = lambda w: w.rearrange("(t p) n -> p t n", p=P)
            keys_t = rows(ctx_t).rearrange("p t (b k) -> p t b k", b=BATCH)
            sp.dma_start(wk[:], rows(w_k)).then_inc(k_params, 16)
            for t in range(DT):
                sp.dma_start(ctx2[:, t, :, 0, :], keys_t[:, t]).then_inc(k_params, 16)
            sp.dma_start(bk[:], b_k).then_inc(k_params, 16)
            sp.dma_start(x_sb[:, 0:TILES, :], x_rows[:, 0:TILES, :]).then_inc(x_first, 16)
            sp.dma_start(wq[:], rows(w_q)).then_inc(q_params, 16)
            sp.dma_start(bq[:], b_q).then_inc(q_params, 16)
            for t in range(DT):
                sp.dma_start(ctx2[:, t, :, 1, :], keys_t[:, t]).then_inc(v_params, 16)
            sp.dma_start(wv[:], rows(w_v)).then_inc(v_params, 16)

            def stack_q(n, parity):
                def bounce(i, t):
                    part, done, bounced = ((q_hi, q_hi_done, q_hi_bounced), (q_lo, q_lo_done, q_lo_bounced))[i]
                    sp.wait_ge(done, DT * n + t + 1)
                    sp.dma_start(q_scratch[parity, i, P * t:P * t + P, :], part[:, t, :]).then_inc(bounced[t], 16)

                def stack(t):
                    for block_row, i, bounced in ((0, 0, q_hi_bounced), (32, 0, q_hi_bounced), (64, 1, q_lo_bounced)):
                        sp.wait_ge(bounced[t], 16 * n + 16)
                        sp.dma_start(q_stack[block_row:block_row + 32, parity, HALF_PAIRS * t:HALF_PAIRS * (t + 1), :],
                                     q_scratch[parity, i, P * t:P * t + P, :].rearrange("(a d) n -> d a n", d=32)
                                     ).then_inc(q_stacked[t], 16)

                bounce(0, 0)
                bounce(1, 0)
                bounce(0, 1)
                stack(0)
                bounce(1, 1)
                stack(1)

            def stack_max(n, parity):
                sp.wait_ge(mxt_sb, n + 1)
                for r in range(2):
                    sp.dma_start(q_stack[MAX_ROW + r:MAX_ROW + r + 1, parity, :, :],
                                 neg_max_t[r:HEADS:2, :]).then_inc(max_stacked, 16)

            def next_v(c, b, g):
                sp.wait_ge(pv_psum, GROUPS * c + (g + 1 + CREDIT["pv_psum"]))
                sp.dma_start(v_cur[0:ROWS, 2 * g:2 * g + 2, :, :, :],
                             v_all[0:ROWS, b + 1, 2 * g:2 * g + 2, :, :, :]).then_inc(v_ready[g], 16)

            sp.wait_ge(k_split, DT)
            for i, part in enumerate((k_hi, k_lo)):
                sp.dma_start(k_scratch[i].rearrange("(t p) n -> p t n", p=P),
                             part[:].rearrange("p t b k -> p t (b k)")).then_inc(k_bounced, 16)
            sp.wait_ge(pool_init, 4)
            sp.wait_ge(k_bounced, 32)
            for block_row, i in ((0, 0), (32, 1), (64, 0)):
                for r in range(2):
                    row = block_row + DH * r
                    sp.dma_start(k_stack[row:row + DH, :, :, r * KEYS:r * KEYS + KEYS],
                                 k_scratch[i].rearrange("(a r d) (b k) -> r d b a k", r=2, d=DH, k=KEYS)[r]
                                 ).then_inc(k_stacked, 16)
            sp.wait_ge(mask_step, 4)
            for b in range(BATCH):
                sp.dma_start(k_stack[MASK_ROW:MASK_ROW + 1, b, :, :].rearrange("q a (r k) -> q (a r) k", r=2),
                             mask_row[0:1, b, :].unsqueeze(1).broadcast_to([1, HEADS, KEYS])).then_inc(k_stacked, 16)
            sp.wait_ge(pool_init, 8)
            sp.wait_ge(zeroed, 1)
            for r in range(2):
                sp.dma_start(k_stack[MAX_ROW + r:MAX_ROW + r + 1, :, :, r * KEYS:r * KEYS + KEYS]
                             .rearrange("q b a k -> q (b a) k"),
                             unit_row[0:1, :].unsqueeze(1).broadcast_to([1, BATCH * PAIRS, KEYS])).then_inc(k_stacked, 16)
            sp.dma_start(q_stack[MASK_ROW:MASK_ROW + 1, :, :, :].rearrange("q s a n -> q (s a) n"),
                         mask_ones[0:1, :].unsqueeze(1).broadcast_to([1, 2 * PAIRS, CHUNK])).then_inc(k_stacked, 16)
            stack_q(0, 0)
            sp.dma_start(x_sb[:, TILES:2 * TILES, :], x_rows[:, TILES:2 * TILES, :]).then_inc(x_second, 16)
            sp.dma_start(wo[:], rows(w_o)).then_inc(o_params, 16)
            sp.wait_ge(v_step, 2 + 4)
            sp.wait_ge(v_done, 2)
            for g in range(GROUPS):
                sp.dma_start(v_cur[0:ROWS, 2 * g:2 * g + 2, :, :, :],
                             v_all[0:ROWS, 0, 2 * g:2 * g + 2, :, :, :]).then_inc(v_ready[g], 16)
            stack_q(1, 1)
            stack_max(0, 0)
            sp.dma_start(x_sb[:, 2 * TILES:, :], x_rows[:, 2 * TILES:, :]).then_inc(x_rest, 16)
            sp.dma_start(wi_gu[:, :, 0, :], rows(w_gate_t)).then_inc(weights_loaded, 16)
            sp.dma_start(wi_gu[:, :, 1, :], rows(w_up_t)).then_inc(weights_loaded, 16)
            sp.dma_start(wi_d[:], rows(w_down_t)).then_inc(weights_loaded, 16)

            def chunk(c, b, j):
                moves_v = j == PER_BATCH - 1 and not peeled(b)
                if moves_v:
                    for g in range(GROUPS - 1):
                        next_v(c, b, g)
                if not (peeled(b) and j == PER_BATCH - 1):
                    stack_max(c + 1, 1 - j)
                if moves_v:
                    next_v(c, b, GROUPS - 1)
                if not peeled(b):
                    stack_q(c + 2, j)

            all_chunks(sp, chunk)

        @block.gpsimd
        def _(pool):
            wide = lambda v: v.rearrange("(a n) -> a n", a=1)
            pool.dma_start(mask_u8[:], mask.unsqueeze(0).broadcast_to([P, BATCH, KEYS])).then_inc(mask_loaded, 16)
            pool.dma_start(gates[:, 0:1], wide(g_xattn).broadcast_to([P, 1])).then_inc(gate_params, 16)
            pool.dma_start(gates[:, 1:2], wide(g_ffn).broadcast_to([P, 1])).then_inc(gate_params, 16)
            pool.dma_start(bv[:], wide(b_v).broadcast_to([P, DIM])).then_inc(bv_loaded, 16)
            pool.dma_start(bo[:], wide(b_o).broadcast_to([P, DIM])).then_inc(gate_params, 16)
            pool.memset(ident[:], 0.0).then_inc(pool_init, 1)
            pool.memset(minus_half[:], -0.5).then_inc(pool_init, 1)
            pool.memset(eps[:], EPS).then_inc(pool_init, 1)
            pool.memset(k_stack[:].rearrange("p b a k -> p (b a k)").bitcast(mybir.dt.uint32), 0).then_inc(pool_init, 1)
            pool.wait_ge(pool_init, 4)
            pool.affine_select(out=ident[:], in_=ident[:], compare_op=ALU.not_equal, fill=1.0, base=0,
                               pattern=[[-1, P]], channel_multiplier=1).then_inc(pool_init, 1)
            pool.memset(head_rows[:], 1.0).then_inc(pool_init, 1)
            pool.memset(ones_col[:], 1.0)
            pool.memset(unit_row[:], MAX_UNIT).then_inc(pool_init, 1)
            pool.memset(mask_ones[:], MASK_ONE).then_inc(pool_init, 1)
            pool.wait_ge(pool_init, 6)
            pool.affine_select(out=head_rows[:, 0:1], in_=head_rows[:, 0:1], compare_op=ALU.is_gt, fill=0.0,
                               base=SPLIT, pattern=[[0, 1]], channel_multiplier=-1).then_inc(pool_init, 1)
            pool.affine_select(out=head_rows[:, 1:2], in_=head_rows[:, 1:2], compare_op=ALU.is_ge, fill=0.0,
                               base=-SPLIT, pattern=[[0, 1]], channel_multiplier=1).then_inc(pool_init, 1)

            def normalise_x(n):
                pool.wait_ge(x_rest, 16)
                pool.wait_ge(pool_step, 2 * n + 2)
                pool.wait_ge(xt_psum, DT * n)
                rows_n = x_sb[:, bass.ds(TILES * (0 if isinstance(n, int) and n == CHUNKS else n), TILES), :]
                pool.tensor_tensor(xh[:], rows_n,
                                   mean_var[:, :, 0:1].broadcast_to([P, TILES, DIM]), ALU.subtract).then_inc(centred, 1)
                pool.wait_ge(centred, n - 1)
                pool.tensor_tensor(xh[:], xh[:], rstd[:].unsqueeze(2).broadcast_to([P, TILES, DIM]),
                                   ALU.mult).then_inc(normed, 1)

            def prepare(n):
                inverse_deviation(pool, n, stats_done, pool_step, var_eps, mean_var, eps, minus_half, rstd)
                if not (isinstance(n, int) and n < 2):
                    normalise_x(n)
                pool.wait_ge(bo_ready, 1)
                pool.wait_ge(normed, n + 1)
                rows_n = x_sb[:, bass.ds(TILES * n, TILES), :]
                pool.tensor_tensor(rows_n, rows_n, bo[:].unsqueeze(1).broadcast_to([P, TILES, DIM]), ALU.add).then_inc(residual_ready, 1)

            prepare(0)
            prepare(1)
            prepare(2)
            pool.wait_ge(weights_loaded, 48)
            pool.tensor_copy(w_gu16[:], wi_gu[:]).then_inc(w_converted, 1)
            pool.tensor_copy(w_d16[:], wi_d[:]).then_inc(w_converted, 1)
            with pool.Fori(0, CHUNKS - 3) as c:
                prepare(c + 3)
            inverse_deviation(pool, CHUNKS, stats_done, pool_step, var_eps, mean_var, eps, minus_half, rstd)
            normalise_x(CHUNKS)

        @block.scalar
        def _(act):
            act.sem_inc(exp_done, CREDIT["exp_done"])
            act.sem_inc(pv_sb, CREDIT["pv_sb"])
            act.wait_ge(q_params, 32)
            act.mul(wq[:], wq[:], QK_SCALE).then_inc(params_ready, 1)
            act.mul(bq[:], bq[:], QK_SCALE).then_inc(params_ready, 1)
            act.wait_ge(params_ready, 2)

            def xt_copy(n, t):
                act.wait_ge(xt_psum, DT * n + t + 1)
                if not first(n):
                    act.wait_ge(q_psum, DT * n)
                act.copy(xh_t[:, t, :], mx_bank[1 + t][:, :]).then_inc(xt_sb, 1)

            def q_copy(n, t):
                act.wait_ge(q_psum, DT * n + t + 1)
                if not first(n):
                    act.wait_ge(q_hi_bounced[t], 16 * n)
                act.activation(q_hi[:, t, :], work[t][:, :], ACT.Identity, bias=bq[:, t:t + 1]).then_inc(q_hi_done, 1)

            def exp_tile(c, i):
                act.wait_ge(st_psum, ST_PER_CHUNK * c + i + 1)
                if i % ST_PER_GROUP == 0:
                    act.wait_ge(pv_psum, GROUPS * c + (i // ST_PER_GROUP - 1 + CREDIT["pv_psum"]))
                n = TILE_ROWS[i % 3]
                act.activation(probs[0:n, i % (2 * ST_PER_GROUP), :], st_bank[i % 2][0:n, :], ACT.Exp,
                               scale=EXP_SCALE).then_inc(exp_done, 1)

            def pv_copy(c, g):
                act.wait_ge(pv_psum, GROUPS * c + (g + 1 + CREDIT["pv_psum"]))
                act.wait_ge(nt_psum, GROUPS * c + (g - 1 + CREDIT["nt_psum"]))
                act.copy(ou[:, g % 2, :], pv_bank[:, :]).then_inc(pv_sb, 1)

            def at_copy(c, t):
                act.wait_ge(at_psum, DT * c + (t + 1 + CREDIT["at_psum"]))
                act.wait_ge(o_psum, 2 * c + CREDIT["o_psum"])
                act.copy(att_t[:, t, :], (work[1], mx_bank[2])[t][:, :]).then_inc(at_sb, 1)

            def prepare_q(n):
                for t in range(DT):
                    xt_copy(n, t)
                for t in range(DT):
                    q_copy(n, t)

            prepare_q(0)
            act.wait_ge(gate_params, 48)
            act.wait_ge(o_params, 16)
            act.activation(att_gate[:], gates[:, 0:1], ACT.Tanh).then_inc(gates_tanh, 1)
            act.activation(ffn_gate[:], gates[:, 1:2], ACT.Tanh).then_inc(gates_tanh, 1)
            act.wait_ge(gates_tanh, 2)
            act.activation(wo[:], wo[:], ACT.Copy, scale=att_gate[:, 0:1]).then_inc(wo_ready, 1)
            act.activation(bo[:], bo[:], ACT.Copy, scale=att_gate[:, 0:1]).then_inc(bo_ready, 1)
            prepare_q(1)
            for i in range(ST_PER_GROUP):
                exp_tile(0, i)

            def chunk(c, b, j):
                for g in range(1, GROUPS):
                    for i in range(ST_PER_GROUP):
                        exp_tile(c, ST_PER_GROUP * g + i)
                        if i == 3:
                            pv_copy(c, g - 1)
                last_chunk = peeled(b) and j == PER_BATCH - 1
                if not peeled(b):
                    for t in range(DT):
                        xt_copy(c + 2, t)
                at_copy(c, 0)
                pv_copy(c, GROUPS - 1)
                if not peeled(b):
                    q_copy(c + 2, 0)
                if not last_chunk:
                    exp_tile(c + 1, 0)
                    exp_tile(c + 1, 1)
                if not peeled(b):
                    q_copy(c + 2, 1)
                if not last_chunk:
                    exp_tile(c + 1, 2)
                    exp_tile(c + 1, 3)
                at_copy(c, 1)
                if not last_chunk:
                    exp_tile(c + 1, 4)
                    exp_tile(c + 1, 5)

            all_chunks(act, chunk)

        @block.vector
        def _(dve):
            dve.sem_inc(mx_reduced, CREDIT["mx_reduced"])
            dve.sem_inc(x1_done, CREDIT["x1_done"])

            def chunk_stats(n):
                row_stats(dve, n, x_sb, stats, mean_var, stats_step, stats_done, normed, waiter)

            def chunk_norm(n):
                normalise_rows(dve, n, x_sb, xh, mean_var, rstd, pool_step, xt_psum, normed)

            dve.memset(q_stack[96:P, :, :, :].rearrange("p s a n -> p (s a n)").bitcast(mybir.dt.uint32), 0).then_inc(zeroed, 1)
            dve.wait_ge(mask_loaded, 16)
            dve.tensor_copy(mask_f[:], mask_u8[:]).then_inc(mask_step, 1)
            dve.wait_ge(mask_step, 1)
            dve.tensor_reduce(some_valid[:], mask_f[:], AX.X, ALU.min).then_inc(mask_step, 1)
            dve.wait_ge(mask_step, 2)
            dve.tensor_scalar(some_valid[:], some_valid[:], -QK_SCALE, QK_SCALE, ALU.mult, ALU.add).then_inc(mask_step, 1)
            dve.wait_ge(mask_step, 3)
            for b in range(BATCH):
                last = dve.tensor_scalar(mask_row[:, b, :], mask_f[:, b, :], some_valid[:, b:b + 1],
                                         -MASK_ONE / QK_SCALE, ALU.mult, ALU.mult)
            last.then_inc(mask_step, 1)
            dve.wait_ge(k_params, 64)
            for t in range(DT):
                for half in range(2):
                    dve.wait_ge(k_psum, 2 * t + half + 1)
                    for b in range(2):
                        last = dve.tensor_scalar(k_f[:, t, 2 * half + b, :],
                                                 st_bank[half][:, b * KEYS:b * KEYS + KEYS], bk[:, t:t + 1],
                                                 some_valid[:, 2 * half + b:2 * half + b + 1], ALU.add, ALU.mult)
                    last.then_inc(k_step, 1)
                dve.wait_ge(k_step, 3 * t + 2)
                dve.tensor_copy(k_hi[:, t], k_f[:, t]).then_inc(k_step, 1)
                dve.wait_ge(k_step, 3 * t + 3)
                dve.tensor_tensor(k_lo[:, t], k_f[:, t], k_hi[:, t], ALU.subtract).then_inc(k_split, 1)
            dve.wait_ge(x_first, 16)
            chunk_stats(0)
            chunk_norm(0)

            def q_low(n, t):
                dve.wait_ge(q_hi_done, DT * n + t + 1)
                if not first(n):
                    dve.wait_ge(q_lo_bounced[t], 16 * n)
                dve.scalar_tensor_tensor(q_lo[:, t, :], work[t][:, :], bq[:, t:t + 1], q_hi[:, t, :],
                                         ALU.add, ALU.subtract).then_inc(q_lo_done, 1)

            dve.memset(v_all[:, :, :, :, 1, :], 1.0)
            dve.memset(v_all[96:P, :, :, 3, 0, :], 0.0).then_inc(v_step, 1)
            dve.memset(v_cur[96:P, :, :, :, :], 0.0).then_inc(zeroed, 1)
            for t in range(DT):
                q_low(0, t)
            dve.memset(probs[96:P, :, :].rearrange("p s n -> p (s n)"), 0.0).then_inc(zeroed, 1)
            dve.wait_ge(x_second, 16)
            chunk_stats(1)

            dve.wait_ge(v_step, 1)
            dve.wait_ge(pool_init, 10)
            dve.wait_ge(bv_loaded, 16)
            bv_heads = bv[:].rearrange("p (a r d) -> p a r d", r=2, d=DH)

            def v_of_batch(b):
                for part, (tile, r) in enumerate(PV_PARTS):
                    m = TILE_ROWS[tile]
                    dve.wait_ge(v_psum, 3 * b + tile + 1)
                    src = v_banks[tile]
                    heads = src[0:m, 0:DIM].rearrange("p (a r d) -> p a r d", r=2, d=DH)[:, :, r, :]
                    dve.tensor_tensor(v_all[0:m, b, :, part, 0, :], heads, bv_heads[0:m, :, r, :],
                                      ALU.add).then_inc(v_step, 1)
                    if tile == 1:
                        dve.wait_ge(v_step, 4 * b + part + 2)
                        both = v_all[0:m, b, :, part, :, :]
                        dve.tensor_scalar(both, both, head_rows[0:m, r:r + 1], None, ALU.mult).then_inc(v_done, 1)

            def max_tile(n, m):
                t, p = max_place(m)
                if m == 0 and not first(n):
                    dve.wait_ge(mxt_psum, n)
                dve.wait_ge(mx_psum, MX * n + m + 1)
                dve.tensor_reduce(neg_max[:, t, 2 * p:2 * p + 2],
                                  mx_bank[m % 3][:, 0:PAIR_KEYS].rearrange("q (r k) -> q r k", r=2),
                                  AX.X, ALU.max, negate=True).then_inc(mx_reduced, 1)

            def max_copy(n):
                dve.wait_ge(mxt_psum, n + 1)
                if not first(n):
                    dve.wait_ge(max_stacked, 16 * 2 * n)
                dve.tensor_scalar(neg_max_t[:, :], mx_bank[0][0:HEADS, :], 1.0 / MAX_UNIT, None,
                                  ALU.mult).then_inc(mxt_sb, 1)

            def normalise(c, g):
                src = nt_bank[g][:, :].rearrange("q (t h e d) -> q t h e d", t=TILES, h=4, e=2)
                dve.wait_ge(nt_psum, GROUPS * c + (g + 1 + CREDIT["nt_psum"]))
                dve.reciprocal(rec[:, g % 2], src[:, :, :, 1, 0]).then_inc(rec_done, 1)
                dve.wait_ge(rec_done, GROUPS * c + g + 1)
                dve.wait_ge(at_psum, DT * c + CREDIT["at_psum"])
                dst = att[:, :, 4 * DH * g:4 * DH * (g + 1)].rearrange("q t (h d) -> q t h d", h=4)
                dve.tensor_tensor(dst, src[:, :, :, 0, :], rec[:, g % 2].unsqueeze(3).broadcast_to([P, TILES, 4, DH]),
                                  ALU.mult).then_inc(att_done, 1)

            def residual(c, u):
                dve.wait_ge(o_psum, 2 * c + (u + 1 + CREDIT["o_psum"]))
                dve.wait_ge(residual_ready, c + 1)
                rows = x_sb[:, bass.ds(TILES * c + 2 * u, 2), :]
                dve.tensor_tensor(rows, rows, work[u][:, :].rearrange("q (t d) -> q t d", t=2),
                                  ALU.add).then_inc(x1_done, 1)

            v_of_batch(0)
            chunk_norm(1)
            for b in range(1, BATCH):
                v_of_batch(b)
            for t in range(DT):
                q_low(1, t)
            for m in range(MX):
                max_tile(0, m)
            max_copy(0)
            dve.wait_ge(x_rest, 16)
            chunk_stats(2)

            def chunk(c, b, j):
                last_chunk = peeled(b) and j == PER_BATCH - 1
                if last_chunk:
                    dve.wait_ge(weights_loaded, 48)
                    dve.tensor_reduce(w_top[:, 0:1], wi_gu[:].rearrange("p t w n -> p (t w n)"), AX.X,
                                      ALU.max, apply_absolute_value=True)
                    dve.tensor_reduce(w_top[:, 1:2], wi_d[:].rearrange("p t n -> p (t n)"), AX.X,
                                      ALU.max, apply_absolute_value=True).then_inc(wide_found, 1)
                    dve.wait_ge(wide_found, 1)
                    dve.tensor_scalar(w_wide[:], w_top[:], NARROW_MAX, None, ALU.is_gt).then_inc(wide_found, 1)
                    dve.wait_ge(wide_counted, 1)
                    dve.tensor_reduce(w_count[:], mx_bank[0][0:1, 0:2], AX.X, ALU.max).then_inc(narrow_set, 1)
                    dve.wait_ge(narrow_set, 1)
                    dve.tensor_scalar(narrow_flag[:], w_count[:], 0.0, None, ALU.is_equal).then_inc(narrow_set, 1)
                for g in range(1, GROUPS):
                    if not last_chunk:
                        for m in range(MX_STEPS[g - 1], MX_STEPS[g]):
                            max_tile(c + 1, m)
                    if g >= 2:
                        normalise(c, g - 2)
                if not last_chunk:
                    max_copy(c + 1)
                normalise(c, 2)
                if not peeled(b):
                    chunk_stats(c + 3)
                    for t in range(DT):
                        q_low(c + 2, t)
                normalise(c, 3)
                for u in range(2):
                    residual(c, u)

            all_chunks(dve, chunk)

        @block.tensor
        def _(pe):
            pe.sem_inc(pv_psum, CREDIT["pv_psum"])
            pe.sem_inc(nt_psum, CREDIT["nt_psum"])
            pe.sem_inc(at_psum, CREDIT["at_psum"])
            pe.sem_inc(o_psum, CREDIT["o_psum"])

            def x_transposes(n, t):
                if t == 0:
                    pe.wait_ge(normed, n + 1)
                for i in range(TILES):
                    last = pe.transpose(mx_bank[1 + t][:, P * i:P * i + P], xh[:, i, P * t:P * t + P], ident[:])
                last.then_inc(xt_psum, 1)

            def q_project(n, t):
                pe.wait_ge(xt_sb, DT * n + DT)
                for k in range(DT):
                    last = pe.matmul(work[t][:, :], wq[:, k, P * t:P * t + P], xh_t[:, k, :],
                                     start=(k == 0), stop=(k == DT - 1))
                last.then_inc(q_psum, 1)

            def max_scores(n, b, parity, m):
                t, p = max_place(m)
                if m % (MX // DT) == 0:
                    pe.wait_ge(q_stacked[m // (MX // DT)], 16 * STACK_DMAS * (n + 1))
                    if m == 0 and not first(n):
                        pe.wait_ge(mxt_sb, n)
                before = m - 3 if m >= 3 else (MX - 2, MX - 1, MX - 3)[m] - MX
                pe.wait_ge(mx_reduced, MX * n + (before + 1 + CREDIT["mx_reduced"]))
                pe.matmul(mx_bank[m % 3][:, 0:PAIR_KEYS], q_stack[0:MAX_ROW, parity, p, P * t:P * t + P],
                          k_stack[0:MAX_ROW, b, p, :], start=True, stop=True).then_inc(mx_psum, 1)

            def max_transposes(n):
                pe.wait_ge(mx_reduced, MX * n + (MX + CREDIT["mx_reduced"]))
                for i in range(TILES):
                    last = pe.transpose(mx_bank[0][0:HEADS, P * i:P * i + P], neg_max[:, i, :], ident[:])
                last.then_inc(mxt_psum, 1)

            def scores(c, b, parity, i):
                if i == 0:
                    pe.wait_ge(max_stacked, 16 * 2 * (c + 1))
                tile, p = i % 3, i // 3
                m = TILE_ROWS[tile]
                pe.wait_ge(exp_done, ST_PER_CHUNK * c + (i - 1 + CREDIT["exp_done"]))
                pe.matmul(st_bank[i % 2][0:m, :], k_stack[:, b, p, ROWS * tile:ROWS * tile + m],
                          q_stack[:, parity, p, :], start=True, stop=True).then_inc(st_psum, 1)

            def values(c, b, g, second):
                if not second:
                    pe.wait_ge(exp_done, ST_PER_CHUNK * c + (ST_PER_GROUP * (g + 1) + CREDIT["exp_done"]))
                    pe.wait_ge(v_ready[g], 16 * b + 16)
                    pe.wait_ge(pv_sb, GROUPS * c + (g + CREDIT["pv_sb"]))
                for p in range(2):
                    for part in (2 * second, 2 * second + 1):
                        tile, r = PV_PARTS[part]
                        at = 32 * (2 * p + r)
                        last = pe.matmul(
                            pv_bank[at:at + 32, :],
                            v_cur[:, 2 * g + p, part, :, :].rearrange("k e d -> k (e d)"),
                            probs[:, (ST_PER_GROUP * g + 3 * p + tile) % (2 * ST_PER_GROUP), :],
                            start=not second, stop=bool(second))
                if second:
                    last.then_inc(pv_psum, 1)

            def norm_transposes(c, g):
                pe.wait_ge(pv_sb, GROUPS * c + (g + 1 + CREDIT["pv_sb"]))
                for i in range(TILES):
                    last = pe.transpose(nt_bank[g][:, P * i:P * i + P], ou[:, g % 2, P * i:P * i + P], ident[:])
                last.then_inc(nt_psum, 1)

            def att_transposes(c, t):
                pe.wait_ge(att_done, GROUPS * c + 2 * t + 2)
                for i in range(TILES):
                    last = pe.transpose((work[1], mx_bank[2])[t][:, P * i:P * i + P], att[:, i, P * t:P * t + P], ident[:])
                last.then_inc(at_psum, 1)

            def out_project(c, u, k):
                if k:
                    pe.wait_ge(at_sb, DT * c + DT)
                for i in range(2):
                    q0 = P * (2 * u + i)
                    last = pe.matmul(work[u][:, DIM * i:DIM * i + DIM], att_t[:, k, q0:q0 + P], wo[:, k, :],
                                     start=(k == 0 and i == 0), stop=bool(k), skip_group_check=True)
                if k:
                    last.then_inc(o_psum, 1)

            def v_project(b):
                for tile in range(3):
                    m = TILE_ROWS[tile]
                    if b:
                        pe.wait_ge(v_step, 1 + 4 * (b - 1) + (1, 3, 4)[tile])
                    keys = ctx2[:, :, b, :, :].rearrange("p t r k -> p t (r k)")
                    for k in range(DT):
                        last = pe.matmul(v_banks[tile][0:m, 0:DIM], keys[:, k, ROWS * tile:ROWS * tile + m], wv[:, k, :],
                                         start=(k == 0), stop=(k == DT - 1))
                    last.then_inc(v_psum, 1)

            pe.wait_ge(k_params, 64)
            for t in range(DT):
                for half in range(2):
                    if t:
                        pe.wait_ge(k_step, half + 1)
                    for k in range(DT):
                        last = pe.matmul(st_bank[half][:, 0:PAIR_KEYS], wk[:, k, P * t:P * t + P],
                                         ctx2[:, k, 2 * half:2 * half + 2, 0, :], start=(k == 0), stop=(k == DT - 1))
                    last.then_inc(k_psum, 1)
            pe.wait_ge(pool_init, 5)
            for t in range(DT):
                x_transposes(0, t)
            pe.wait_ge(params_ready, 2)
            for t in range(DT):
                q_project(0, t)
            pe.wait_ge(v_params, 48)
            v_project(0)
            for t in range(DT):
                x_transposes(1, t)
            for b in range(1, BATCH):
                v_project(b)
            pe.wait_ge(q_lo_done, DT)
            for t in range(DT):
                q_project(1, t)
            pe.wait_ge(k_stacked, 16 * K_STACK_DMAS)
            pe.wait_ge(zeroed, 3)
            pe.wait_ge(v_step, 1 + 4 * BATCH)
            for m in range(MX):
                max_scores(0, 0, 0, m)
            max_transposes(0)
            for i in range(ST_PER_GROUP):
                scores(0, 0, 0, i)
            pe.wait_ge(mxt_sb, 1)
            pe.wait_ge(wo_ready, 1)

            def chunk(c, b, j):
                n, nb, nj = c + 1, (b if j == 0 else b + 1), 1 - j
                last_chunk = peeled(b) and j == PER_BATCH - 1
                for g in range(1, GROUPS):
                    if last_chunk and g == 2:
                        pe.wait_ge(wide_found, 2)
                        pe.matmul(mx_bank[0][0:1, 0:2], ones_col[:], w_wide[:], start=True,
                                  stop=True).then_inc(wide_counted, 1)
                    i = ST_PER_GROUP * g
                    m0, m1 = MX_STEPS[g - 1], MX_STEPS[g]
                    order = list(range(m0, m1))

                    def maxes(count):
                        for _ in range(count):
                            if order and not last_chunk:
                                max_scores(n, nb, nj, order.pop(0))

                    for s in range(2):
                        scores(c, b, j, i + 2 * s)
                        maxes(1)
                        scores(c, b, j, i + 2 * s + 1)
                        maxes(2)
                        values(c, b, g - 1, s)
                        maxes(1)
                    scores(c, b, j, i + 4)
                    maxes(1)
                    scores(c, b, j, i + 5)
                    maxes(1)
                    if g >= 2:
                        pe.wait_ge(x1_done, 2 * c + (g - 3 + CREDIT["x1_done"]))
                        norm_transposes(c, g - 2)
                    maxes(MX)
                values(c, b, GROUPS - 1, 0)
                if not last_chunk:
                    max_transposes(n)
                pe.wait_ge(att_done, GROUPS * c + 1)
                norm_transposes(c, 2)
                if not peeled(b):
                    for t in range(DT):
                        x_transposes(c + 2, t)
                att_transposes(c, 0)
                values(c, b, GROUPS - 1, 1)
                if not peeled(b):
                    pe.wait_ge(att_done, GROUPS * c + 3)
                    q_project(c + 2, 0)
                if not last_chunk:
                    scores(n, nb, nj, 0)
                    scores(n, nb, nj, 1)
                pe.wait_ge(at_sb, DT * c + 1)
                if not peeled(b):
                    q_project(c + 2, 1)
                norm_transposes(c, 3)
                if not last_chunk:
                    scores(n, nb, nj, 2)
                    scores(n, nb, nj, 3)
                if not peeled(b):
                    pe.wait_ge(q_lo_done, DT * (c + 2) + 1)
                else:
                    pe.wait_ge(att_done, GROUPS * c + 3)
                out_project(c, 0, 0)
                att_transposes(c, 1)
                if not peeled(b):
                    pe.wait_ge(q_lo_done, DT * (c + 2) + 2)
                out_project(c, 1, 0)
                if not last_chunk:
                    scores(n, nb, nj, 4)
                out_project(c, 0, 1)
                if not last_chunk:
                    scores(n, nb, nj, 5)
                out_project(c, 1, 1)

            all_chunks(pe, chunk)


def feed_forward(nc, st, sb, sem, out_rows, x_sb, ident, ffn_gate, wi_gu, wi_d, stats, mean_var,
                 var_eps, eps, minus_half, rstd, xh, xh_t):
    def f_sb(name, shape, dtype=F32):
        return sb(name, shape, dtype, st)

    def f_sem(name):
        return sem(name, st)

    w_gu = f_sb("w_gu", [P, DT, 2, HIDDEN])
    w_d = f_sb("w_d", [P, HT, DIM])
    waiter = f_sb("f_waiter", [P, 1])
    silu = f_sb("silu", [P, 2, CHUNK])
    hidden = f_sb("hidden", [P, 2, HT, CHUNK])
    out_gate = f_sb("out_gate", [P, 1])

    def bank(name):
        return st.enter_context(nc.psum_tensor(name, [P, 512], F32))

    xt_bank = [bank(f"xt_bank{i}") for i in range(2)]
    gate_bank = [bank(f"gate_bank{i}") for i in range(2)]
    up_bank = [bank(f"up_bank{i}") for i in range(2)]
    down_bank = [bank(f"down_bank{i}") for i in range(2)]

    w_ready = f_sem("w_ready")
    stats_step = f_sem("f_stats_step")
    stats_done = f_sem("f_stats_done")
    pool_step = f_sem("f_pool_step")
    normed = f_sem("f_normed")
    xt_psum = f_sem("f_xt_psum")
    xt_sb = f_sem("f_xt_sb")
    gate_psum = f_sem("gate_psum")
    up_psum = f_sem("up_psum")
    silu_done = f_sem("silu_done")
    hidden_done = f_sem("hidden_done")
    down_psum = f_sem("down_psum")
    y_done = f_sem("y_done")
    stored = f_sem("stored")

    Y_CREDIT = 2

    def loop(engine, chunk):
        chunk(0, 0)
        with engine.Fori(0, (CHUNKS - 2) // 2) as i:
            for j in range(2):
                chunk(2 * i + 1 + j, 1 - j)
        chunk(CHUNKS - 1, (CHUNKS - 1) % 2)

    with nc.Block() as block:

        @block.sync
        def _(sp):
            def chunk(c, parity):
                sp.wait_ge(y_done, 2 * c + (2 + Y_CREDIT))
                rows = bass.ds(TILES * c, TILES)
                sp.dma_start(out_rows[:, rows, :], x_sb[:, rows, :]).then_inc(stored, 16)
            loop(sp, chunk)
            sp.wait_ge(stored, 16 * CHUNKS)

        @block.gpsimd
        def _(pool):
            pool.sem_inc(pool_step, 2)
            with pool.Fori(0, CHUNKS - 1) as c:
                inverse_deviation(pool, c + 1, stats_done, pool_step, var_eps, mean_var, eps, minus_half, rstd)

        @block.scalar
        def _(act):
            act.activation(w_gu[:], wi_gu[:], ACT.Copy, scale=WEIGHT_SCALE).then_inc(w_ready, 1)

            def chunk(c, parity):
                for t in range(DT):
                    act.wait_ge(xt_psum, DT * c + t + 1)
                    if not first(c) and t == 0:
                        act.wait_ge(up_psum, HT * c)
                    act.copy(xh_t[:, t, :], xt_bank[t][:, :]).then_inc(xt_sb, 1)
                for h in range(HT):
                    act.wait_ge(gate_psum, HT * c + h + 1)
                    if not (first(c) and h < 2):
                        act.wait_ge(hidden_done, HT * c + h - 1)
                    act.activation(silu[:, h % 2, :], gate_bank[h % 2][:, :], ACT.Silu).then_inc(silu_done, 1)
            loop(act, chunk)

        @block.vector
        def _(dve):
            dve.sem_inc(y_done, Y_CREDIT)
            for done in (stats_step, stats_done, normed):
                dve.sem_inc(done, 1)
            dve.tensor_scalar(w_d[:], wi_d[:], WEIGHT_SCALE, None, ALU.mult).then_inc(w_ready, 1)

            def chunk_stats(n):
                row_stats(dve, n, x_sb, stats, mean_var, stats_step, stats_done, normed, waiter)

            def chunk_norm(n):
                normalise_rows(dve, n, x_sb, xh, mean_var, rstd, pool_step, xt_psum, normed)

            def residual(c, u):
                dve.wait_ge(down_psum, 2 * c + u + 1)
                rows = x_sb[:, bass.ds(TILES * c + 2 * u, 2), :]
                dve.scalar_tensor_tensor(rows, down_bank[u][:, :].rearrange("q (t d) -> q t d", t=2),
                                         ffn_gate[:, 0:1], rows, ALU.mult, ALU.add).then_inc(y_done, 1)

            def chunk(c, parity):
                last_chunk = isinstance(c, int) and c == CHUNKS - 1
                if not last_chunk:
                    chunk_stats(c + 1)
                    chunk_norm(c + 1)
                for h in range(HT):
                    dve.wait_ge(up_psum, HT * c + h + 1)
                    dve.wait_ge(silu_done, HT * c + h + 1)
                    dve.tensor_tensor(hidden[:, parity, h, :], up_bank[h % 2][:, :], silu[:, h % 2, :],
                                      ALU.mult).then_inc(hidden_done, 1)
                    if h == 2 and not first(c):
                        for u in range(2):
                            residual(c - 1, u)
                if last_chunk:
                    for u in range(2):
                        residual(c, u)
            loop(dve, chunk)

        @block.tensor
        def _(pe):
            pe.wait_ge(w_ready, 2)

            def x_transposes(n):
                if not first(n):
                    pe.wait_ge(normed, n + 1)
                for t in range(DT):
                    if not first(n):
                        pe.wait_ge(xt_sb, DT * n)
                    for i in range(TILES):
                        last = pe.transpose(xt_bank[t][:, P * i:P * i + P], xh[:, i, P * t:P * t + P], ident[:])
                    last.then_inc(xt_psum, 1)

            def gate_up(c, h):
                if not (first(c) and h < 2):
                    pe.wait_ge(hidden_done, HT * c + h - 1)
                for which, (banks, done) in enumerate(((gate_bank, gate_psum), (up_bank, up_psum))):
                    for k in range(DT):
                        last = pe.matmul(banks[h % 2][:, :], w_gu[:, k, which, P * h:P * h + P], xh_t[:, k, :],
                                         start=(k == 0), stop=(k == DT - 1))
                    last.then_inc(done, 1)

            def down(c, parity, u):
                pe.wait_ge(hidden_done, HT * c + HT)
                pe.wait_ge(y_done, 2 * c + (u - 1 + Y_CREDIT))
                for i in range(2):
                    q0 = P * (2 * u + i)
                    for h in range(HT):
                        last = pe.matmul(down_bank[u][:, DIM * i:DIM * i + DIM], hidden[:, parity, h, q0:q0 + P],
                                         w_d[:, h, :], start=(h == 0), stop=(h == HT - 1))
                last.then_inc(down_psum, 1)

            x_transposes(0)

            def chunk(c, parity):
                pe.wait_ge(xt_sb, DT * c + DT)
                for h in range(HT):
                    gate_up(c, h)
                    if h == 1 and not first(c):
                        for u in range(2):
                            down(c - 1, 1 - parity, u)
                if isinstance(c, int) and c == CHUNKS - 1:
                    for u in range(2):
                        down(c, parity, u)
                else:
                    x_transposes(c + 1)
            loop(pe, chunk)


def feed_forward_narrow(nc, st, sb, sem, out_rows, x_sb, ident, ffn_gate, w_gu, w_d, stats, mean_var,
                        var_eps, eps, minus_half, rstd, xh):
    def f_sb(name, shape, dtype=F32):
        return sb("n_" + name, shape, dtype, st)

    def f_sem(name):
        return sem("n_" + name, st)

    waiter = f_sb("waiter", [P, 1])
    xt_hi = f_sb("xt_hi", [P, 2, DT, CHUNK], F16)
    xt_lo = f_sb("xt_lo", [P, 2, DT, CHUNK], F16)
    silu = f_sb("silu", [P, 2, CHUNK])
    hidden = f_sb("hidden", [P, 2, CHUNK])
    h_hi = f_sb("h_hi", [P, 2, HT, CHUNK], F16)
    h_lo = f_sb("h_lo", [P, 2, HT, CHUNK], F16)
    out_gate = f_sb("out_gate", [P, 1])

    def bank(name):
        return st.enter_context(nc.psum_tensor("n_" + name, [P, 512], F32))

    xt_bank = [bank(f"xt_bank{i}") for i in range(2)]
    gate_bank = [bank(f"gate_bank{i}") for i in range(2)]
    up_bank = [bank(f"up_bank{i}") for i in range(2)]
    down_bank = [bank(f"down_bank{i}") for i in range(2)]

    gate_ready = f_sem("gate_ready")
    stats_step = f_sem("stats_step")
    stats_done = f_sem("stats_done")
    pool_step = f_sem("pool_step")
    normed = f_sem("normed")
    xt_psum = f_sem("xt_psum")
    xt_hi_done = f_sem("xt_hi_done")
    xt_lo_done = f_sem("xt_lo_done")
    gate_psum = f_sem("gate_psum")
    up_psum = f_sem("up_psum")
    silu_done = f_sem("silu_done")
    hidden_done = f_sem("hidden_done")
    h_hi_done = f_sem("h_hi_done")
    h_lo_done = f_sem("h_lo_done")
    down_psum = f_sem("down_psum")
    y_done = f_sem("y_done")
    stored = f_sem("stored")

    Y_CREDIT = 2

    def loop(engine, chunk):
        chunk(0, 0)
        with engine.Fori(0, (CHUNKS - 2) // 2) as i:
            for j in range(2):
                chunk(2 * i + 1 + j, 1 - j)
        chunk(CHUNKS - 1, (CHUNKS - 1) % 2)

    with nc.Block() as block:

        @block.sync
        def _(sp):
            def chunk(c, parity):
                sp.wait_ge(y_done, 2 * c + (2 + Y_CREDIT))
                rows = bass.ds(TILES * c, TILES)
                sp.dma_start(out_rows[:, rows, :], x_sb[:, rows, :]).then_inc(stored, 16)
            loop(sp, chunk)
            sp.wait_ge(stored, 16 * CHUNKS)

        @block.gpsimd
        def _(pool):
            pool.sem_inc(pool_step, 2)
            with pool.Fori(0, CHUNKS - 1) as c:
                inverse_deviation(pool, c + 1, stats_done, pool_step, var_eps, mean_var, eps, minus_half, rstd)

        @block.scalar
        def _(act):
            act.mul(out_gate[:], ffn_gate[:], WEIGHT_SCALE / HIDDEN_SCALE).then_inc(gate_ready, 1)

            def x_high(n, parity):
                for t in range(DT):
                    act.wait_ge(xt_psum, DT * n + t + 1)
                    if not (isinstance(n, int) and n < 2) and t == 0:
                        act.wait_ge(up_psum, HT * (n - 1))
                    act.activation(xt_hi[:, parity, t, :], xt_bank[t][:, :], ACT.Copy, scale=X_SCALE).then_inc(xt_hi_done, 1)

            def high(c, parity, h):
                act.wait_ge(hidden_done, HT * c + h + 1)
                if h == 0 and not (isinstance(c, int) and c < 2):
                    act.wait_ge(down_psum, 2 * (c - 1))
                act.copy(h_hi[:, parity, h, :], hidden[:, h % 2, :]).then_inc(h_hi_done, 1)

            x_high(0, 0)

            def chunk(c, parity):
                for h in range(HT):
                    act.wait_ge(gate_psum, HT * c + h + 1)
                    if not (first(c) and h < 2):
                        act.wait_ge(hidden_done, HT * c + h - 1)
                    act.activation(silu[:, h % 2, :], gate_bank[h % 2][:, :], ACT.Silu,
                                   scale=WEIGHT_SCALE / X_SCALE).then_inc(silu_done, 1)
                    if h >= 1:
                        high(c, parity, h - 1)
                    if h == 2 and not (isinstance(c, int) and c == CHUNKS - 1):
                        x_high(c + 1, 1 - parity)
                high(c, parity, HT - 1)
            loop(act, chunk)

        @block.vector
        def _(dve):
            dve.sem_inc(y_done, Y_CREDIT)
            for done in (stats_step, stats_done, normed):
                dve.sem_inc(done, 1)

            def chunk_stats(n):
                row_stats(dve, n, x_sb, stats, mean_var, stats_step, stats_done, normed, waiter)

            def chunk_norm(n):
                normalise_rows(dve, n, x_sb, xh, mean_var, rstd, pool_step, xt_psum, normed)

            def x_low(n, parity):
                for t in range(DT):
                    dve.wait_ge(xt_hi_done, DT * n + t + 1)
                    dve.scalar_tensor_tensor(xt_lo[:, parity, t, :], xt_bank[t][:, :], X_SCALE, xt_hi[:, parity, t, :],
                                             ALU.mult, ALU.subtract).then_inc(xt_lo_done, 1)

            def low(c, parity, h):
                dve.wait_ge(h_hi_done, HT * c + h + 1)
                dve.tensor_tensor(h_lo[:, parity, h, :], hidden[:, h % 2, :], h_hi[:, parity, h, :],
                                  ALU.subtract).then_inc(h_lo_done, 1)

            def residual(c, u):
                dve.wait_ge(down_psum, 2 * c + u + 1)
                rows = x_sb[:, bass.ds(TILES * c + 2 * u, 2), :]
                dve.scalar_tensor_tensor(rows, down_bank[u][:, :].rearrange("q (t d) -> q t d", t=2),
                                         out_gate[:, 0:1], rows, ALU.mult, ALU.add).then_inc(y_done, 1)

            x_low(0, 0)
            dve.wait_ge(gate_ready, 1)

            def chunk(c, parity):
                last_chunk = isinstance(c, int) and c == CHUNKS - 1
                for h in range(HT):
                    dve.wait_ge(up_psum, HT * c + h + 1)
                    dve.wait_ge(silu_done, HT * c + h + 1)
                    if not (first(c) and h < 2):
                        dve.wait_ge(h_lo_done, HT * c + h - 1)
                    dve.scalar_tensor_tensor(hidden[:, h % 2, :], up_bank[h % 2][:, :],
                                             HIDDEN_SCALE * WEIGHT_SCALE / X_SCALE, silu[:, h % 2, :],
                                             ALU.mult, ALU.mult).then_inc(hidden_done, 1)
                    if h == 0 and not last_chunk:
                        chunk_stats(c + 1)
                    if h >= 1:
                        low(c, parity, h - 1)
                    if h == 1 and not last_chunk:
                        chunk_norm(c + 1)
                    if h in (3, 4) and not first(c):
                        residual(c - 1, h - 3)
                    if h == 2 and not last_chunk:
                        x_low(c + 1, 1 - parity)
                low(c, parity, HT - 1)
                if last_chunk:
                    for u in range(2):
                        residual(c, u)
            loop(dve, chunk)

        @block.tensor
        def _(pe):
            def x_transposes(n):
                if not first(n):
                    pe.wait_ge(normed, n + 1)
                for t in range(DT):
                    if not first(n):
                        pe.wait_ge(xt_lo_done, DT * n)
                    for i in range(TILES):
                        last = pe.transpose(xt_bank[t][:, P * i:P * i + P], xh[:, i, P * t:P * t + P], ident[:])
                    last.then_inc(xt_psum, 1)

            def gate_up(c, parity, h):
                if not (first(c) and h < 2):
                    pe.wait_ge(hidden_done, HT * c + h - 1)
                for which, (banks, done) in enumerate(((gate_bank, gate_psum), (up_bank, up_psum))):
                    for part in (xt_hi, xt_lo):
                        for k in range(DT):
                            last = pe.matmul(banks[h % 2][:, :], w_gu[:, k, which, P * h:P * h + P], part[:, parity, k, :],
                                             start=(part is xt_hi and k == 0), stop=(part is xt_lo and k == DT - 1))
                    last.then_inc(done, 1)

            def down(c, parity, u):
                pe.wait_ge(h_lo_done, HT * c + HT)
                pe.wait_ge(y_done, 2 * c + (u - 1 + Y_CREDIT))
                for i in range(2):
                    q0 = P * (2 * u + i)
                    for h in range(HT):
                        for part in (h_hi, h_lo):
                            last = pe.matmul(down_bank[u][:, DIM * i:DIM * i + DIM], part[:, parity, h, q0:q0 + P],
                                             w_d[:, h, :], start=(h == 0 and part is h_hi),
                                             stop=(h == HT - 1 and part is h_lo))
                last.then_inc(down_psum, 1)

            x_transposes(0)

            def chunk(c, parity):
                last_chunk = isinstance(c, int) and c == CHUNKS - 1
                pe.wait_ge(xt_hi_done, DT * c + DT)
                pe.wait_ge(xt_lo_done, DT * c + DT)
                for h in range(HT):
                    gate_up(c, parity, h)
                    if h == 2 and not last_chunk:
                        x_transposes(c + 1)
                    if h in (1, 2) and not first(c):
                        down(c - 1, 1 - parity, h - 1)
                if last_chunk:
                    for u in range(2):
                        down(c, parity, u)
            loop(pe, chunk)


def kernel(**inputs):
    import numpy as _np
    import concourse.bacc as _bacc
    from concourse import mybir as _mybir
    from concourse.bass_utils import run_bass_kernel_spmd as _run

    a = {k: _np.asarray(v) for k, v in inputs.items()}
    ctx = a["ctx_1024"]
    laid_out = {
        "x": a["x"],
        "ctx_t": ctx.reshape(-1, ctx.shape[-1]).T,
        "mask": a["mask_BxS2_bk0"],
        "g_xattn": a["g_xattn"],
        "g_ffn": a["g_ffn"],
        "w_q": a["L0_xattn_W_Q"], "b_q": a["L0_xattn_b_Q"].reshape(DT, P).T,
        "w_k": a["L0_xattn_W_K"], "b_k": a["L0_xattn_b_K"].reshape(DT, P).T,
        "w_v": a["L0_xattn_W_V"], "b_v": a["L0_xattn_b_V"],
        "w_o": a["L0_xattn_W_O"], "b_o": a["L0_xattn_b_O"],
        "w_gate_t": a["L0_ffn_w_gate"].T,
        "w_up_t": a["L0_ffn_w_up"].T,
        "w_down_t": a["L0_ffn_w_down"].T,
    }
    nc = _bacc.Bacc("TRN2", target_bir_lowering=False, num_devices=1)
    arrays, args = {}, []
    for name, value in laid_out.items():
        value = _np.ascontiguousarray(value)
        arrays[f"in_{name}_dram"] = value
        args.append(nc.dram_tensor(f"in_{name}_dram", value.shape, _mybir.dt.from_np(value.dtype), kind="ExternalInput").ap())
    out = nc.dram_tensor("out_0_dram", a["x"].shape, _mybir.dt.float32, kind="ExternalOutput").ap()
    flamingo_block(nc, *args, out)
    r = _run(nc, [arrays], core_ids=[0])
    return r.results[0]["out_0_dram"]
```

```python
from contextlib import ExitStack

import concourse.bass as bass
from concourse import mybir

ALU = mybir.AluOpType
ACT = mybir.ActivationFunctionType
AX = mybir.AxisListType
F32 = mybir.dt.float32
F16 = mybir.dt.float16
I32 = mybir.dt.int32
U8 = mybir.dt.uint8

P = 128
EPS = 1e-5
WEIGHT_SCALE = 1.0 / 127.0

BATCH, SEQ, DIM = 4, 1024, 256
KEYS = 154
HEADS = 16
DH = DIM // HEADS
HIDDEN = 768

CHUNK = 512
TILES = CHUNK // P
CHUNKS = BATCH * SEQ // CHUNK
PER_BATCH = SEQ // CHUNK
DT = DIM // P
HT = HIDDEN // P
PAIRS = HEADS // 2
GROUPS = PAIRS // 2
PAIR_KEYS = 2 * KEYS
HALF_PAIRS = PAIRS // DT
ROWS = 103
TILE_ROWS = [ROWS, ROWS, PAIR_KEYS - 2 * ROWS]
SPLIT = KEYS - ROWS
ST_PER_GROUP = 2 * len(TILE_ROWS)
ST_PER_CHUNK = GROUPS * ST_PER_GROUP
PV_PARTS = [(0, 0), (1, 1), (1, 0), (2, 1)]

QK_SCALE = 16.0
Q_PARTS = 1
MASK_ROW = 3 * 32
MAX_ROW = P - 2
MASK_ONE = 32768.0
MAX_UNIT = 4096.0
EXP_SCALE = 1.0 / (QK_SCALE * QK_SCALE * DH ** 0.5)

NARROW_MAX = 127.0
X_SCALE = 1024.0
HIDDEN_SCALE = 0.25

STACK_DMAS = 3

K_STACK_DMAS = 3 * 2
FIXED_ROW_DMAS = 3


def flamingo_block(nc, x, ctx_t, mask, g_xattn, g_ffn, w_q, b_q, w_k, b_k, w_v, b_v, w_o, b_o,
                   w_gate_t, w_up_t, w_down_t, out):
    x_rows = x.rearrange("b (n p) d -> p (b n) d", p=P)
    out_rows = out.rearrange("b (n p) d -> p (b n) d", p=P)

    with ExitStack() as ctx:
        def sb(name, shape, dtype=F32, stack=ctx):
            return stack.enter_context(nc.sbuf_tensor(name, shape, dtype))

        def sem(name, stack=ctx):
            return stack.enter_context(nc.semaphore(name))

        x_sb = sb("x_sb", [P, CHUNKS * TILES, DIM])
        ident = sb("ident", [P, P])
        ffn_gate = sb("ffn_gate", [P, 1])
        wi_gu = sb("wi_gu", [P, DT, 2, HIDDEN], I32)
        wi_d = sb("wi_d", [P, HT, DIM], I32)
        stats = sb("stats", [P, TILES, 6])
        mean_var = sb("mean_var", [P, TILES, 2])
        var_eps = sb("var_eps", [P, TILES])
        minus_half = sb("minus_half", [P, TILES])
        eps = sb("eps", [P, TILES])
        rstd = sb("rstd", [P, TILES])
        xh = sb("xh", [P, TILES, DIM])
        xh_t = sb("xh_t", [P, DT, CHUNK])
        xt_hi = sb("xt_hi", [P, 2, DT, CHUNK], F16)
        xt_lo = sb("xt_lo", [P, 2, DT, CHUNK], F16)
        weights_loaded = sem("weights_loaded")
        w_gu16 = sb("w_gu16", [P, DT, 2, HIDDEN], F16)
        w_d16 = sb("w_d16", [P, HT, DIM], F16)
        narrow_flag = sb("narrow_flag", [1, 1], I32)

        with ExitStack() as att_stack:
            attention(nc, att_stack, sb, sem, x_rows, x_sb, ident, ffn_gate, wi_gu, wi_d, stats,
                      mean_var, var_eps, eps, minus_half, rstd, xh, xh_t, weights_loaded,
                      w_gu16, w_d16, narrow_flag, xt_hi, xt_lo, ctx_t, mask, g_xattn, g_ffn,
                      w_q, b_q, w_k, b_k, w_v, b_v, w_o, b_o, w_gate_t, w_up_t, w_down_t)
        narrow = nc.values_load(narrow_flag[0:1, 0:1], min_val=0, max_val=1)
        with nc.If(narrow != 0):
            with ExitStack() as ffn_stack:
                feed_forward_narrow(nc, ffn_stack, sb, sem, out_rows, x_sb, ident, ffn_gate, w_gu16, w_d16,
                                    stats, mean_var, var_eps, eps, minus_half, rstd, xh, xt_hi, xt_lo)
        with nc.Else():
            with ExitStack() as ffn_stack:
                feed_forward(nc, ffn_stack, sb, sem, out_rows, x_sb, ident, ffn_gate, wi_gu, wi_d, stats,
                             mean_var, var_eps, eps, minus_half, rstd, xh, xh_t)


def first(n):
    return isinstance(n, int) and n == 0


def inverse_deviation(pool, n, stats_done, pool_step, var_eps, mean_var, eps, minus_half, rstd):
    pool.wait_ge(stats_done, n + 1)
    pool.tensor_tensor(var_eps[:], mean_var[:, :, 1], eps[:], ALU.add).then_inc(pool_step, 1)
    pool.wait_ge(pool_step, 2 * n + 1)
    pool.tensor_tensor(rstd[:], var_eps[:], minus_half[:], ALU.pow).then_inc(pool_step, 1)


def row_stats(dve, n, x_sb, stats, mean_var, stats_step, stats_done, normed, waiter):
    if not first(n):
        dve.wait_ge(normed, n)
    for t in range(TILES):
        last = dve.bn_stats(stats[:, t, :], x_sb[:, (TILES * n + t) % (TILES * CHUNKS), :])
    last.then_inc(stats_step, 1)
    dve.wait_ge(stats_step, n + 1)
    dve.tensor_copy(waiter[:], stats[:, 0, 0:1])
    for t in range(TILES):
        last = dve.bn_aggr(mean_var[:, t, :], stats[:, t, :])
    last.then_inc(stats_done, 1)


def normalise_rows(dve, n, x_sb, xh, mean_var, rstd, pool_step, xt_psum, normed):
    dve.wait_ge(pool_step, 2 * n + 2)
    if not first(n):
        dve.wait_ge(xt_psum, DT * n)
    for t in range(TILES):
        last = dve.tensor_scalar(xh[:, t, :], x_sb[:, TILES * n + t, :], mean_var[:, t, 0:1],
                                 rstd[:, t:t + 1], ALU.subtract, ALU.mult)
    last.then_inc(normed, 1)


def attention(nc, st, sb, sem, x_rows, x_sb, ident, ffn_gate, wi_gu, wi_d, stats, mean_var, var_eps,
              eps, minus_half, rstd, xh, xh_t, weights_loaded, w_gu16, w_d16, narrow_flag,
              xt_hi, xt_lo, ctx_t, mask, g_xattn, g_ffn,
              w_q, b_q, w_k, b_k, w_v, b_v, w_o, b_o, w_gate_t, w_up_t, w_down_t):
    def a_sb(name, shape, dtype=F32):
        return sb(name, shape, dtype, st)

    def a_sem(name):
        return sem(name, st)

    wq = a_sb("wq", [P, DT, DIM])
    wq_hi = a_sb("wq_hi", [P, DT, DIM], F16)
    wq_lo = a_sb("wq_lo", [P, DT, DIM], F16)
    wk = a_sb("wk", [P, DT, DIM])
    wv = a_sb("wv", [P, DT, DIM])
    wo = a_sb("wo", [P, DT, DIM])
    bq = a_sb("bq", [P, DT])
    bk = a_sb("bk", [P, DT])
    bv = a_sb("bv", [P, DT])
    bv_wide = a_sb("bv_wide", [P, DT, P])
    bo = a_sb("bo", [P, DIM])
    gates = a_sb("gates", [P, 2])
    att_gate = a_sb("att_gate", [P, 1])
    ctx2 = a_sb("ctx2", [P, DT, BATCH, 2, KEYS])
    mask_u8 = a_sb("mask_u8", [P, BATCH, KEYS], U8)
    mask_f = a_sb("mask_f", [P, BATCH, KEYS])
    some_valid = a_sb("some_valid", [P, BATCH])
    mask_row = a_sb("mask_row", [P, BATCH, KEYS], F16)
    mask_ones = a_sb("mask_ones", [P, CHUNK], F16)
    unit_row = a_sb("unit_row", [P, KEYS], F16)
    q_scratch = nc.dram_tensor("q_scratch", (2, 2, DIM, CHUNK), F16).ap()
    k_scratch = nc.dram_tensor("k_scratch", (2, DIM, BATCH * KEYS), F16).ap()
    k_f = a_sb("k_f", [P, BATCH, KEYS])
    k_hi = a_sb("k_hi", [P, DT, BATCH, KEYS], F16)
    k_lo = a_sb("k_lo", [P, DT, BATCH, KEYS], F16)
    k_stack = a_sb("k_stack", [P, DT, BATCH, HALF_PAIRS, PAIR_KEYS], F16)
    v_all = a_sb("v_all", [P, BATCH, PAIRS, 4, 2, DH])
    v_cur = a_sb("v_cur", [P, PAIRS, 4, 2, DH])
    head_rows = a_sb("head_rows", [P, 2])
    q_hi = a_sb("q_hi", [P, DT, CHUNK], F16)
    q_lo = a_sb("q_lo", [P, DT, CHUNK], F16)
    q_stack = a_sb("q_stack", [P, 2, PAIRS, CHUNK], F16)
    waiter = a_sb("waiter", [P, 1])
    neg_max = a_sb("neg_max", [P, TILES, HEADS])
    neg_max_t = a_sb("neg_max_t", [HEADS, CHUNK], F16)
    w_top = a_sb("w_top", [P, 2])
    w_wide = a_sb("w_wide", [P, 2])
    ones_col = a_sb("ones_col", [P, 1])
    w_count = a_sb("w_count", [1, 1])
    probs = a_sb("probs", [P, 2 * ST_PER_GROUP, CHUNK])
    ou = a_sb("ou", [P, 2, CHUNK])
    rec = a_sb("rec", [P, 2, TILES, 4])
    att = a_sb("att", [P, TILES, DIM])
    att_t = a_sb("att_t", [P, DT, CHUNK])

    def bank(name):
        return st.enter_context(nc.psum_tensor(name, [P, 512], F32))

    work = [bank(f"work{i}") for i in range(2)]
    mx_bank = [bank(f"mx_bank{i}") for i in range(3)]
    st_bank = [bank(f"st_bank{i}") for i in range(2)]
    pv_bank = bank("pv_bank")

    k_params = a_sem("k_params")
    q_params = a_sem("q_params")
    v_params = a_sem("v_params")
    o_params = a_sem("o_params")
    mask_loaded = a_sem("mask_loaded")
    gate_params = a_sem("gate_params")
    x_first = a_sem("x_first")
    x_second = a_sem("x_second")
    x_third = a_sem("x_third")
    x_rest = a_sem("x_rest")
    pool_init = a_sem("pool_init")
    k_zeroed = a_sem("k_zeroed")
    zeroed = a_sem("zeroed")
    fixed_values = a_sem("fixed_values")
    fixed_rows = a_sem("fixed_rows")
    mask_rows = a_sem("mask_rows")
    v_fixed = a_sem("v_fixed")
    params_ready = a_sem("params_ready")
    wq_split = a_sem("wq_split")
    wo_ready = a_sem("wo_ready")
    bv_ready = a_sem("bv_ready")
    bo_psum = a_sem("bo_psum")
    bo_ready = a_sem("bo_ready")
    gates_tanh = a_sem("gates_tanh")
    mask_step = a_sem("mask_step")
    k_psum = a_sem("k_psum")
    k_step = a_sem("k_step")
    k_split = a_sem("k_split")
    v_psum = a_sem("v_psum")
    v_step = a_sem("v_step")
    k_bounced = [a_sem(f"k_bounced{t}") for t in range(DT)]
    k_stacked = [a_sem(f"k_stacked{t}") for t in range(DT)]
    stats_done = a_sem("stats_done")
    stats_step = a_sem("stats_step")
    pool_step = a_sem("pool_step")
    centred = a_sem("centred")
    normed = a_sem("normed")
    residual_ready = a_sem("residual_ready")
    xt_psum = a_sem("xt_psum")
    xt_hi_done = a_sem("xt_hi_done")
    xt_lo_done = a_sem("xt_lo_done")
    q_psum = a_sem("q_psum")
    q_hi_done = a_sem("q_hi_done")
    q_lo_done = a_sem("q_lo_done")
    q_hi_bounced = [a_sem(f"q_hi_bounced{t}") for t in range(DT)]
    q_lo_bounced = [a_sem(f"q_lo_bounced{t}") for t in range(DT)]
    q_stacked = [a_sem(f"q_stacked{t}") for t in range(DT)]
    mx_psum = a_sem("mx_psum")
    mx_reduced = a_sem("mx_reduced")
    mxt_psum = a_sem("mxt_psum")
    mxt_sb = a_sem("mxt_sb")
    max_stacked = a_sem("max_stacked")
    w_converted = a_sem("w_converted")
    wide_found = a_sem("wide_found")
    wide_counted = a_sem("wide_counted")
    narrow_set = a_sem("narrow_set")
    next_hi_done = a_sem("next_hi_done")
    next_lo_done = a_sem("next_lo_done")
    st_psum = a_sem("st_psum")
    exp_done = a_sem("exp_done")
    v_ready = [a_sem(f"v_ready{g}") for g in range(GROUPS)]
    pv_psum = a_sem("pv_psum")
    pv_sb = a_sem("pv_sb")
    nt_psum = a_sem("nt_psum")
    rec_done = a_sem("rec_done")
    att_done = a_sem("att_done")
    at_psum = a_sem("at_psum")
    at_sb = a_sem("at_sb")
    o_psum = a_sem("o_psum")
    x1_done = a_sem("x1_done")

    next_bank = st_bank

    def xt_banks(n):
        if isinstance(n, int) and n == CHUNKS:
            return next_bank
        return work if isinstance(n, int) and n == 1 else mx_bank[1:]

    nt_bank = [work[0], work[1], work[0], mx_bank[1]]
    v_banks = [st_bank[0], st_bank[1], pv_bank]
    MX = TILES * PAIRS
    MX_STEPS = [0, 11, 21, MX]
    XT1_LOW_AT = (13, 15)
    Q1_LOW_AT = (23, 27)
    CREDIT = {"mx_reduced": 3, "exp_done": 2, "pv_psum": 2, "pv_sb": 2, "nt_psum": 2, "at_psum": DT,
              "o_psum": 2, "x1_done": 2}

    def all_chunks(engine, chunk):
        with engine.Fori(0, BATCH - 1) as b:
            for j in range(PER_BATCH):
                chunk(b * PER_BATCH + j, b, j)
        for j in range(PER_BATCH):
            chunk((BATCH - 1) * PER_BATCH + j, BATCH - 1, j)

    def max_place(m):
        half, rest = divmod(m, TILES * HALF_PAIRS)
        t, p = divmod(rest, HALF_PAIRS)
        return t, half * HALF_PAIRS + p

    def peeled(b):
        return isinstance(b, int)

    with nc.Block() as block:

        @block.sync
        def _(sp):
            rows = lambda w: w.rearrange("(t p) n -> p t n", p=P)
            keys_t = rows(ctx_t).rearrange("p t (b k) -> p t b k", b=BATCH)
            wide = lambda v: v.rearrange("(a n) -> a n", a=1)
            sp.dma_start(x_sb[:, 0:TILES, :], x_rows[:, 0:TILES, :]).then_inc(x_first, 16)
            sp.dma_start(wk[:], rows(w_k)).then_inc(k_params, 16)
            for t in range(DT):
                sp.dma_start(ctx2[:, t, :, 0, :], keys_t[:, t]).then_inc(k_params, 16)
            sp.dma_start(bk[:], b_k).then_inc(k_params, 16)
            sp.dma_start(wq[:], rows(w_q)).then_inc(q_params, 16)
            sp.dma_start(bq[:], b_q).then_inc(q_params, 16)
            sp.dma_start(x_sb[:, TILES:2 * TILES, :], x_rows[:, TILES:2 * TILES, :]).then_inc(x_second, 16)

            def bounce_q(n, parity, i, t):
                part, done, bounced = ((q_hi, q_hi_done, q_hi_bounced), (q_lo, q_lo_done, q_lo_bounced))[i]
                sp.wait_ge(done, DT * n + t + 1)
                sp.dma_start(q_scratch[parity, i, P * t:P * t + P, :], part[:, t, :]).then_inc(bounced[t], 16)

            def stack_half(n, parity, t):
                for block_row, i, bounced in ((0, 0, q_hi_bounced), (32, 0, q_hi_bounced), (64, 1, q_lo_bounced)):
                    sp.wait_ge(bounced[t], 16 * n + 16)
                    sp.dma_start(q_stack[block_row:block_row + 32, parity, HALF_PAIRS * t:HALF_PAIRS * (t + 1), :],
                                 q_scratch[parity, i, P * t:P * t + P, :].rearrange("(a d) n -> d a n", d=32)
                                 ).then_inc(q_stacked[t], 16)

            def stack_q(n, parity):
                bounce_q(n, parity, 0, 0)
                bounce_q(n, parity, 1, 0)
                bounce_q(n, parity, 0, 1)
                stack_half(n, parity, 0)
                bounce_q(n, parity, 1, 1)
                stack_half(n, parity, 1)

            def stack_max(n, parity):
                sp.wait_ge(mxt_sb, n + 1)
                for r in range(2):
                    sp.dma_start(q_stack[MAX_ROW + r:MAX_ROW + r + 1, parity, :, :],
                                 neg_max_t[r:HEADS:2, :]).then_inc(max_stacked, 16)

            def next_v(c, b, g):
                sp.wait_ge(pv_psum, GROUPS * c + (g + 1 + CREDIT["pv_psum"]))
                sp.dma_start(v_cur[0:ROWS, 2 * g:2 * g + 2, :, :, :],
                             v_all[0:ROWS, b + 1, 2 * g:2 * g + 2, :, :, :]).then_inc(v_ready[g], 16)

            def bounce_k(t):
                sp.wait_ge(k_split, t + 1)
                for i, part in enumerate((k_hi, k_lo)):
                    sp.dma_start(k_scratch[i, P * t:P * t + P, :],
                                 part[:, t].rearrange("p b k -> p (b k)")).then_inc(k_bounced[t], 16)

            def stack_k(t, block_row, i):
                sp.wait_ge(k_bounced[t], 32)
                sp.wait_ge(k_zeroed, 1)
                for r in range(2):
                    row = block_row + DH * r
                    for_pairs = k_scratch[i, P * t:P * t + P, :].rearrange("(a r d) (b k) -> r d b a k", r=2, d=DH, k=KEYS)
                    sp.dma_start(k_stack[row:row + DH, t, :, :, r * KEYS:r * KEYS + KEYS],
                                 for_pairs[r]).then_inc(k_stacked[t], 16)

            bounce_k(0)
            for t in range(DT):
                sp.dma_start(ctx2[:, t, :, 1, :], keys_t[:, t]).then_inc(v_params, 16)
            sp.dma_start(wv[:], rows(w_v)).then_inc(v_params, 16)
            stack_k(0, 0, 0)
            bounce_q(0, 0, 0, 0)
            bounce_q(0, 0, 1, 0)
            stack_k(0, 64, 0)
            stack_k(0, 32, 1)
            stack_half(0, 0, 0)
            bounce_k(1)
            bounce_q(0, 0, 0, 1)
            bounce_q(0, 0, 1, 1)
            for block_row, i in ((0, 0), (32, 1), (64, 0)):
                stack_k(1, block_row, i)
            stack_half(0, 0, 1)
            sp.dma_start(wo[:], rows(w_o)).then_inc(o_params, 16)
            sp.dma_start(bv[:], b_v).then_inc(o_params, 16)
            for g, gate in enumerate((g_xattn, g_ffn)):
                sp.dma_start(gates[:, g:g + 1], wide(gate).broadcast_to([P, 1])).then_inc(gate_params, 16)
            sp.dma_start(bo[:], wide(b_o).broadcast_to([P, DIM])).then_inc(gate_params, 16)
            sp.dma_start(x_sb[:, 2 * TILES:3 * TILES, :], x_rows[:, 2 * TILES:3 * TILES, :]).then_inc(x_third, 16)
            sp.wait_ge(v_step, 4)
            sp.wait_ge(v_fixed, 4)
            sp.wait_ge(zeroed, 2)
            for g in range(GROUPS):
                sp.dma_start(v_cur[0:ROWS, 2 * g:2 * g + 2, :, :, :],
                             v_all[0:ROWS, 0, 2 * g:2 * g + 2, :, :, :]).then_inc(v_ready[g], 16)
            bounce_q(1, 1, 0, 0)
            bounce_q(1, 1, 1, 0)
            bounce_q(1, 1, 0, 1)
            stack_half(1, 1, 0)
            bounce_q(1, 1, 1, 1)
            stack_max(0, 0)
            stack_half(1, 1, 1)
            sp.dma_start(x_sb[:, 3 * TILES:, :], x_rows[:, 3 * TILES:, :]).then_inc(x_rest, 16)
            sp.dma_start(wi_gu[:, :, 0, :], rows(w_gate_t)).then_inc(weights_loaded, 16)
            sp.dma_start(wi_gu[:, :, 1, :], rows(w_up_t)).then_inc(weights_loaded, 16)
            sp.dma_start(wi_d[:], rows(w_down_t)).then_inc(weights_loaded, 16)

            def chunk(c, b, j):
                moves_v = j == PER_BATCH - 1 and not peeled(b)
                if moves_v:
                    for g in range(GROUPS - 1):
                        next_v(c, b, g)
                if not (peeled(b) and j == PER_BATCH - 1):
                    stack_max(c + 1, 1 - j)
                if moves_v:
                    next_v(c, b, GROUPS - 1)
                if not peeled(b):
                    stack_q(c + 2, j)

            all_chunks(sp, chunk)

        @block.gpsimd
        def _(pool):
            pool.dma_start(mask_u8[:], mask.unsqueeze(0).broadcast_to([P, BATCH, KEYS])).then_inc(mask_loaded, 16)
            pool.memset(ident[:], 0.0).then_inc(pool_init, 1)
            pool.memset(minus_half[:], -0.5).then_inc(pool_init, 1)
            pool.memset(eps[:], EPS).then_inc(pool_init, 1)
            pool.wait_ge(pool_init, 3)
            pool.affine_select(out=ident[:], in_=ident[:], compare_op=ALU.not_equal, fill=1.0, base=0,
                               pattern=[[-1, P]], channel_multiplier=1).then_inc(pool_init, 1)
            pool.memset(k_stack[:].rearrange("p t b a k -> p (t b a k)").bitcast(mybir.dt.uint32), 0).then_inc(k_zeroed, 1)
            inverse_deviation(pool, 0, stats_done, pool_step, var_eps, mean_var, eps, minus_half, rstd)
            pool.wait_ge(pool_step, 2)
            pool.memset(q_stack[96:P, :, :, :].rearrange("p s a n -> p (s a n)").bitcast(mybir.dt.uint32), 0).then_inc(zeroed, 1)
            pool.wait_ge(zeroed, 1)
            pool.memset(unit_row[:], MAX_UNIT).then_inc(fixed_values, 1)
            pool.memset(mask_ones[:], MASK_ONE).then_inc(fixed_values, 1)
            pool.wait_ge(fixed_values, 2)
            pool.wait_ge(k_zeroed, 1)
            for r in range(2):
                pool.dma_start(k_stack[MAX_ROW + r:MAX_ROW + r + 1, :, :, :, r * KEYS:r * KEYS + KEYS]
                               .rearrange("q t b a k -> q (t b a) k"),
                               unit_row[0:1, :].unsqueeze(1).broadcast_to([1, BATCH * PAIRS, KEYS])).then_inc(fixed_rows, 16)
            pool.dma_start(q_stack[MASK_ROW:MASK_ROW + 1, :, :, :].rearrange("q s a n -> q (s a) n"),
                           mask_ones[0:1, :].unsqueeze(1).broadcast_to([1, 2 * PAIRS, CHUNK])).then_inc(fixed_rows, 16)
            pool.memset(head_rows[:], 1.0).then_inc(pool_init, 1)
            pool.memset(ones_col[:], 1.0)
            pool.wait_ge(pool_init, 5)
            pool.affine_select(out=head_rows[:, 0:1], in_=head_rows[:, 0:1], compare_op=ALU.is_gt, fill=0.0,
                               base=SPLIT, pattern=[[0, 1]], channel_multiplier=-1).then_inc(pool_init, 1)
            pool.affine_select(out=head_rows[:, 1:2], in_=head_rows[:, 1:2], compare_op=ALU.is_ge, fill=0.0,
                               base=-SPLIT, pattern=[[0, 1]], channel_multiplier=1).then_inc(pool_init, 1)
            pool.wait_ge(pool_init, 7)
            for b in range(BATCH):
                last = pool.memset(v_all[96:P, b, :, 3, 0, :], 0.0)
            last.then_inc(v_fixed, 1)

            def normalise_x(n):
                pool.wait_ge({1: x_second, 2: x_third}.get(n, x_rest) if isinstance(n, int) else x_rest, 16)
                pool.wait_ge(pool_step, 2 * n + 2)
                pool.wait_ge(xt_psum, DT * n)
                rows_n = x_sb[:, bass.ds(TILES * (0 if isinstance(n, int) and n == CHUNKS else n), TILES), :]
                pool.tensor_tensor(xh[:], rows_n,
                                   mean_var[:, :, 0:1].broadcast_to([P, TILES, DIM]), ALU.subtract).then_inc(centred, 1)
                pool.wait_ge(centred, n)
                pool.tensor_tensor(xh[:], xh[:], rstd[:].unsqueeze(2).broadcast_to([P, TILES, DIM]),
                                   ALU.mult).then_inc(normed, 1)

            def add_bias(n):
                pool.wait_ge(bo_ready, 1)
                pool.wait_ge(normed, n + 1)
                rows_n = x_sb[:, bass.ds(TILES * n, TILES), :]
                pool.tensor_tensor(rows_n, rows_n, bo[:].unsqueeze(1).broadcast_to([P, TILES, DIM]), ALU.add).then_inc(residual_ready, 1)

            def prepare(n):
                inverse_deviation(pool, n, stats_done, pool_step, var_eps, mean_var, eps, minus_half, rstd)
                normalise_x(n)
                add_bias(n)

            pool.wait_ge(v_fixed, 1)
            inverse_deviation(pool, 1, stats_done, pool_step, var_eps, mean_var, eps, minus_half, rstd)
            normalise_x(1)
            for b in range(BATCH):
                last = pool.memset(v_all[:, b, :, :, 1, :], 1.0)
            last.then_inc(v_fixed, 1)
            pool.wait_ge(v_fixed, 2)
            for part, (tile, r) in enumerate(PV_PARTS):
                if tile == 1:
                    for b in range(BATCH):
                        ones = v_all[:, b, :, part, 1, :]
                        last = pool.affine_select(out=ones, in_=ones, compare_op=ALU.is_ge if r else ALU.is_gt, fill=0.0,
                                                  base=-SPLIT if r else SPLIT, pattern=[[0, PAIRS], [0, DH]],
                                                  channel_multiplier=1 if r else -1)
                    last.then_inc(v_fixed, 1)
            pool.wait_ge(v_fixed, 4)
            pool.memset(v_cur[96:P, :, :, :, :], 0.0).then_inc(zeroed, 1)
            pool.memset(probs[96:P, :, :].rearrange("p s n -> p (s n)"), 0.0).then_inc(zeroed, 1)
            pool.wait_ge(zeroed, 3)
            add_bias(0)
            add_bias(1)
            prepare(2)
            pool.wait_ge(weights_loaded, 48)
            pool.tensor_copy(w_gu16[:], wi_gu[:]).then_inc(w_converted, 1)
            pool.tensor_copy(w_d16[:], wi_d[:]).then_inc(w_converted, 1)
            with pool.Fori(0, CHUNKS - 3) as c:
                prepare(c + 3)
            inverse_deviation(pool, CHUNKS, stats_done, pool_step, var_eps, mean_var, eps, minus_half, rstd)
            normalise_x(CHUNKS)

        @block.scalar
        def _(act):
            act.sem_inc(exp_done, CREDIT["exp_done"])
            act.sem_inc(pv_sb, CREDIT["pv_sb"])
            act.wait_ge(q_params, 32)
            act.mul(wq[:], wq[:], QK_SCALE).then_inc(params_ready, 1)
            act.mul(bq[:], bq[:], QK_SCALE).then_inc(params_ready, 1)
            act.wait_ge(params_ready, 2)
            act.copy(wq_hi[:], wq[:]).then_inc(params_ready, 1)

            def xt_copy(n, t):
                act.wait_ge(xt_psum, DT * n + t + 1)
                if not first(n):
                    act.wait_ge(q_psum, DT * n)
                act.copy(xt_hi[:, Q_PARTS, t, :], xt_banks(n)[t][:, :]).then_inc(xt_hi_done, 1)

            def q_copy(n, t):
                act.wait_ge(q_psum, DT * n + t + 1)
                if not first(n):
                    act.wait_ge(q_hi_bounced[t], 16 * n)
                act.activation(q_hi[:, t, :], work[t][:, :], ACT.Identity, bias=bq[:, t:t + 1]).then_inc(q_hi_done, 1)

            def exp_tile(c, i):
                act.wait_ge(st_psum, ST_PER_CHUNK * c + i + 1)
                if i % ST_PER_GROUP == 0:
                    act.wait_ge(pv_psum, GROUPS * c + (i // ST_PER_GROUP - 1 + CREDIT["pv_psum"]))
                n = TILE_ROWS[i % 3]
                act.activation(probs[0:n, i % (2 * ST_PER_GROUP), :], st_bank[i % 2][0:n, :], ACT.Exp,
                               scale=EXP_SCALE).then_inc(exp_done, 1)

            def pv_copy(c, g):
                act.wait_ge(pv_psum, GROUPS * c + (g + 1 + CREDIT["pv_psum"]))
                act.wait_ge(nt_psum, GROUPS * c + (g - 1 + CREDIT["nt_psum"]))
                act.copy(ou[:, g % 2, :], pv_bank[:, :]).then_inc(pv_sb, 1)

            def at_copy(c, t):
                act.wait_ge(at_psum, DT * c + (t + 1 + CREDIT["at_psum"]))
                act.wait_ge(o_psum, 2 * c + CREDIT["o_psum"])
                act.copy(att_t[:, t, :], (work[1], mx_bank[2])[t][:, :]).then_inc(at_sb, 1)

            def prepare_q(n):
                for t in range(DT):
                    xt_copy(n, t)
                for t in range(DT):
                    q_copy(n, t)

            def v_copies(b):
                for part, (tile, r) in enumerate(PV_PARTS):
                    m = TILE_ROWS[tile]
                    act.wait_ge(v_psum, 3 * b + tile + 1)
                    heads = v_banks[tile][0:m, 0:DIM].rearrange("p (a r d) -> p a r d", r=2, d=DH)[:, :, r, :]
                    act.activation(v_all[0:m, b, :, part, 0, :], heads, ACT.Copy,
                                   scale=head_rows[0:m, r:r + 1] if tile == 1 else 1.0).then_inc(v_step, 1)

            def mask_rows_of(t):
                act.wait_ge(mask_step, 4)
                act.wait_ge(k_zeroed, 1)
                for b in range(BATCH):
                    last = act.copy(k_stack[MASK_ROW:MASK_ROW + 1, t, b, :, :].rearrange("q a (r k) -> q (a r) k", r=2),
                                    mask_row[MASK_ROW:MASK_ROW + 1, b, :].unsqueeze(1).broadcast_to([1, HEADS // DT, KEYS]))
                last.then_inc(mask_rows, 1)

            for t in range(DT):
                xt_copy(0, t)
            q_copy(0, 0)
            mask_rows_of(0)
            q_copy(0, 1)
            act.wait_ge(pool_init, 7)
            act.wait_ge(v_fixed, 1)
            v_copies(0)
            v_copies(1)
            mask_rows_of(1)
            prepare_q(1)
            v_copies(2)
            act.wait_ge(gate_params, 48)
            act.wait_ge(o_params, 32)
            act.activation(att_gate[:], gates[:, 0:1], ACT.Tanh).then_inc(gates_tanh, 1)
            act.activation(ffn_gate[:], gates[:, 1:2], ACT.Tanh).then_inc(gates_tanh, 1)
            for t in range(DT):
                last = act.copy(bv_wide[:, t, :], bv[:, t:t + 1].broadcast_to([P, P]))
            last.then_inc(bv_ready, 1)
            act.wait_ge(gates_tanh, 2)
            act.activation(wo[:], wo[:], ACT.Copy, scale=att_gate[:, 0:1]).then_inc(wo_ready, 1)
            v_copies(3)
            act.wait_ge(zeroed, 3)
            for i in range(ST_PER_GROUP):
                exp_tile(0, i)

            def chunk(c, b, j):
                for g in range(1, GROUPS):
                    for i in range(ST_PER_GROUP):
                        exp_tile(c, ST_PER_GROUP * g + i)
                        if i == 3:
                            pv_copy(c, g - 1)
                last_chunk = peeled(b) and j == PER_BATCH - 1
                if not peeled(b):
                    for t in range(DT):
                        xt_copy(c + 2, t)
                at_copy(c, 0)
                pv_copy(c, GROUPS - 1)
                if last_chunk:
                    for t in range(DT):
                        act.wait_ge(xt_psum, DT * CHUNKS + t + 1)
                        act.copy(xh_t[:, t, :], next_bank[t][:, :])
                        act.activation(xt_hi[:, 0, t, :], next_bank[t][:, :], ACT.Copy, scale=X_SCALE).then_inc(next_hi_done, 1)
                if not peeled(b):
                    q_copy(c + 2, 0)
                    exp_tile(c + 1, 0)
                    exp_tile(c + 1, 1)
                    q_copy(c + 2, 1)
                    exp_tile(c + 1, 2)
                    exp_tile(c + 1, 3)
                    exp_tile(c + 1, 4)
                    at_copy(c, 1)
                    exp_tile(c + 1, 5)
                    return
                at_copy(c, 1)
                if not last_chunk:
                    for i in range(ST_PER_GROUP):
                        exp_tile(c + 1, i)

            all_chunks(act, chunk)

        @block.vector
        def _(dve):
            dve.sem_inc(mx_reduced, CREDIT["mx_reduced"])
            dve.sem_inc(x1_done, CREDIT["x1_done"])

            def chunk_stats(n):
                row_stats(dve, n, x_sb, stats, mean_var, stats_step, stats_done, normed, waiter)

            def chunk_norm(n):
                normalise_rows(dve, n, x_sb, xh, mean_var, rstd, pool_step, xt_psum, normed)

            dve.wait_ge(x_first, 16)
            chunk_stats(0)
            dve.wait_ge(mask_loaded, 16)
            dve.tensor_copy(mask_f[:], mask_u8[:]).then_inc(mask_step, 1)
            dve.wait_ge(mask_step, 1)
            dve.tensor_reduce(some_valid[:], mask_f[:], AX.X, ALU.min).then_inc(mask_step, 1)
            dve.wait_ge(mask_step, 2)
            dve.tensor_scalar(some_valid[:], some_valid[:], -QK_SCALE, QK_SCALE, ALU.mult, ALU.add).then_inc(mask_step, 1)
            dve.wait_ge(mask_step, 3)
            for b in range(BATCH):
                last = dve.tensor_scalar(mask_row[:, b, :], mask_f[:, b, :], some_valid[:, b:b + 1],
                                         -MASK_ONE / QK_SCALE, ALU.mult, ALU.mult)
            last.then_inc(mask_step, 1)
            chunk_norm(0)
            dve.wait_ge(params_ready, 3)
            dve.tensor_tensor(wq_lo[:], wq[:], wq_hi[:], ALU.subtract).then_inc(wq_split, 1)

            def xt_low(n, t):
                dve.wait_ge(xt_hi_done, DT * n + t + 1)
                if not first(n):
                    dve.wait_ge(q_psum, DT * n)
                dve.tensor_tensor(xt_lo[:, Q_PARTS, t, :], xt_banks(n)[t][:, :], xt_hi[:, Q_PARTS, t, :],
                                  ALU.subtract).then_inc(xt_lo_done, 1)

            def split_k(t):
                dve.wait_ge(k_params, 64)
                if t:
                    dve.wait_ge(k_split, t)
                for half in range(2):
                    dve.wait_ge(k_psum, 2 * t + half + 1)
                    for b in range(2):
                        last = dve.tensor_scalar(k_f[:, 2 * half + b, :],
                                                 st_bank[half][:, b * KEYS:b * KEYS + KEYS], bk[:, t:t + 1],
                                                 some_valid[:, 2 * half + b:2 * half + b + 1], ALU.add, ALU.mult)
                    last.then_inc(k_step, 1)
                dve.wait_ge(k_step, 3 * t + 2)
                dve.tensor_copy(k_hi[:, t], k_f[:]).then_inc(k_step, 1)
                dve.wait_ge(k_step, 3 * t + 3)
                dve.tensor_tensor(k_lo[:, t], k_f[:], k_hi[:, t], ALU.subtract).then_inc(k_split, 1)

            def q_low(n, t):
                dve.wait_ge(q_hi_done, DT * n + t + 1)
                if not first(n):
                    dve.wait_ge(q_lo_bounced[t], 16 * n)
                dve.scalar_tensor_tensor(q_lo[:, t, :], work[t][:, :], bq[:, t:t + 1], q_hi[:, t, :],
                                         ALU.add, ALU.subtract).then_inc(q_lo_done, 1)

            split_k(0)
            for t in range(DT):
                xt_low(0, t)
            q_low(0, 0)
            split_k(1)
            q_low(0, 1)
            dve.wait_ge(x_second, 16)
            chunk_stats(1)

            def max_tile(n, m):
                t, p = max_place(m)
                if m == 0 and not first(n):
                    dve.wait_ge(mxt_psum, n)
                dve.wait_ge(mx_psum, MX * n + m + 1)
                dve.tensor_reduce(neg_max[:, t, 2 * p:2 * p + 2],
                                  mx_bank[m % 3][:, 0:PAIR_KEYS].rearrange("q (r k) -> q r k", r=2),
                                  AX.X, ALU.max, negate=True).then_inc(mx_reduced, 1)

            def max_copy(n):
                dve.wait_ge(mxt_psum, n + 1)
                if not first(n):
                    dve.wait_ge(max_stacked, 16 * 2 * n)
                dve.tensor_scalar(neg_max_t[:, :], mx_bank[0][0:HEADS, :], 1.0 / MAX_UNIT, None,
                                  ALU.mult).then_inc(mxt_sb, 1)

            def normalise(c, g):
                src = nt_bank[g][:, :].rearrange("q (t h e d) -> q t h e d", t=TILES, h=4, e=2)
                dve.wait_ge(nt_psum, GROUPS * c + (g + 1 + CREDIT["nt_psum"]))
                dve.reciprocal(rec[:, g % 2], src[:, :, :, 1, 0]).then_inc(rec_done, 1)
                dve.wait_ge(rec_done, GROUPS * c + g + 1)
                dve.wait_ge(at_psum, DT * c + CREDIT["at_psum"])
                dst = att[:, :, 4 * DH * g:4 * DH * (g + 1)].rearrange("q t (h d) -> q t h d", h=4)
                dve.tensor_tensor(dst, src[:, :, :, 0, :], rec[:, g % 2].unsqueeze(3).broadcast_to([P, TILES, 4, DH]),
                                  ALU.mult).then_inc(att_done, 1)

            def residual(c, u):
                dve.wait_ge(o_psum, 2 * c + (u + 1 + CREDIT["o_psum"]))
                dve.wait_ge(residual_ready, c + 1)
                rows = x_sb[:, bass.ds(TILES * c + 2 * u, 2), :]
                dve.tensor_tensor(rows, rows, work[u][:, :].rearrange("q (t d) -> q t d", t=2),
                                  ALU.add).then_inc(x1_done, 1)

            for m in range(MX):
                max_tile(0, m)
                if m in XT1_LOW_AT:
                    xt_low(1, XT1_LOW_AT.index(m))
                if m in Q1_LOW_AT:
                    q_low(1, Q1_LOW_AT.index(m))
            max_copy(0)
            dve.wait_ge(bo_psum, 1)
            dve.wait_ge(gates_tanh, 2)
            dve.scalar_tensor_tensor(bo[:], bo[:], att_gate[:, 0:1], pv_bank[:, 0:DIM], ALU.mult,
                                     ALU.add).then_inc(bo_ready, 1)
            dve.wait_ge(x_third, 16)
            chunk_stats(2)

            def chunk(c, b, j):
                last_chunk = peeled(b) and j == PER_BATCH - 1
                if last_chunk:
                    dve.wait_ge(weights_loaded, 48)
                    dve.tensor_reduce(w_top[:, 0:1], wi_gu[:].rearrange("p t w n -> p (t w n)"), AX.X,
                                      ALU.max, apply_absolute_value=True)
                    dve.tensor_reduce(w_top[:, 1:2], wi_d[:].rearrange("p t n -> p (t n)"), AX.X,
                                      ALU.max, apply_absolute_value=True).then_inc(wide_found, 1)
                    dve.wait_ge(wide_found, 1)
                    dve.tensor_scalar(w_wide[:], w_top[:], NARROW_MAX, None, ALU.is_gt).then_inc(wide_found, 1)
                for g in range(1, GROUPS):
                    if not last_chunk:
                        for m in range(MX_STEPS[g - 1], MX_STEPS[g]):
                            max_tile(c + 1, m)
                    if g >= 2:
                        normalise(c, g - 2)
                normalise(c, 2)
                if not last_chunk:
                    max_copy(c + 1)
                if not peeled(b):
                    for t in range(DT):
                        xt_low(c + 2, t)
                    dve.wait_ge(x_rest, 16)
                    chunk_stats(c + 3)
                    for t in range(DT):
                        q_low(c + 2, t)
                if last_chunk:
                    dve.wait_ge(wide_counted, 1)
                    dve.tensor_reduce(w_count[:], mx_bank[0][0:1, 0:2], AX.X, ALU.max).then_inc(narrow_set, 1)
                    dve.wait_ge(narrow_set, 1)
                    dve.tensor_scalar(narrow_flag[:], w_count[:], 0.0, None, ALU.is_equal).then_inc(narrow_set, 1)
                normalise(c, 3)
                if last_chunk:
                    for t in range(DT):
                        dve.wait_ge(next_hi_done, t + 1)
                        dve.scalar_tensor_tensor(xt_lo[:, 0, t, :], next_bank[t][:, :], X_SCALE, xt_hi[:, 0, t, :],
                                                 ALU.mult, ALU.subtract).then_inc(next_lo_done, 1)
                for u in range(2):
                    residual(c, u)

            all_chunks(dve, chunk)

        @block.tensor
        def _(pe):
            pe.sem_inc(pv_psum, CREDIT["pv_psum"])
            pe.sem_inc(nt_psum, CREDIT["nt_psum"])
            pe.sem_inc(at_psum, CREDIT["at_psum"])
            pe.sem_inc(o_psum, CREDIT["o_psum"])

            def x_transposes(n, t):
                if t == 0:
                    pe.wait_ge(normed, n + 1)
                for i in range(TILES):
                    last = pe.transpose(xt_banks(n)[t][:, P * i:P * i + P], xh[:, i, P * t:P * t + P], ident[:])
                last.then_inc(xt_psum, 1)

            def q_project(n, t, ks=range(DT)):
                pe.wait_ge(xt_hi_done, DT * n + DT)
                pe.wait_ge(xt_lo_done, DT * n + DT)
                for k in ks:
                    passes = ((wq_hi, xt_hi), (wq_hi, xt_lo), (wq_lo, xt_hi))
                    for i, (w, x_part) in enumerate(passes):
                        last = pe.matmul(work[t][:, :], w[:, k, P * t:P * t + P], x_part[:, Q_PARTS, k, :],
                                         start=(k == 0 and i == 0), stop=(k == DT - 1 and i == len(passes) - 1))
                if DT - 1 in ks:
                    last.then_inc(q_psum, 1)

            def max_scores(n, b, parity, m):
                t, p = max_place(m)
                if m % (MX // DT) == 0:
                    pe.wait_ge(q_stacked[m // (MX // DT)], 16 * STACK_DMAS * (n + 1))
                    if m == 0 and not first(n):
                        pe.wait_ge(mxt_sb, n)
                before = m - 3 if m >= 3 else (MX - 2, MX - 1, MX - 3)[m] - MX
                pe.wait_ge(mx_reduced, MX * n + (before + 1 + CREDIT["mx_reduced"]))
                pe.matmul(mx_bank[m % 3][:, 0:PAIR_KEYS], q_stack[0:MAX_ROW, parity, p, P * t:P * t + P],
                          k_stack[0:MAX_ROW, p // HALF_PAIRS, b, p % HALF_PAIRS, :], start=True, stop=True).then_inc(mx_psum, 1)

            def max_transposes(n):
                pe.wait_ge(mx_reduced, MX * n + (MX + CREDIT["mx_reduced"]))
                for i in range(TILES):
                    last = pe.transpose(mx_bank[0][0:HEADS, P * i:P * i + P], neg_max[:, i, :], ident[:])
                last.then_inc(mxt_psum, 1)

            def scores(c, b, parity, i):
                if i == 0:
                    pe.wait_ge(max_stacked, 16 * 2 * (c + 1))
                tile, p = i % 3, i // 3
                m = TILE_ROWS[tile]
                pe.wait_ge(exp_done, ST_PER_CHUNK * c + (i - 1 + CREDIT["exp_done"]))
                pe.matmul(st_bank[i % 2][0:m, :], k_stack[:, p // HALF_PAIRS, b, p % HALF_PAIRS, ROWS * tile:ROWS * tile + m],
                          q_stack[:, parity, p, :], start=True, stop=True).then_inc(st_psum, 1)

            def values(c, b, g, second):
                if not second:
                    pe.wait_ge(exp_done, ST_PER_CHUNK * c + (ST_PER_GROUP * (g + 1) + CREDIT["exp_done"]))
                    pe.wait_ge(v_ready[g], 16 * b + 16)
                    pe.wait_ge(pv_sb, GROUPS * c + (g + CREDIT["pv_sb"]))
                for p in range(2):
                    for part in (2 * second, 2 * second + 1):
                        tile, r = PV_PARTS[part]
                        at = 32 * (2 * p + r)
                        last = pe.matmul(
                            pv_bank[at:at + 32, :],
                            v_cur[:, 2 * g + p, part, :, :].rearrange("k e d -> k (e d)"),
                            probs[:, (ST_PER_GROUP * g + 3 * p + tile) % (2 * ST_PER_GROUP), :],
                            start=not second, stop=bool(second))
                if second:
                    last.then_inc(pv_psum, 1)

            def norm_transposes(c, g):
                pe.wait_ge(pv_sb, GROUPS * c + (g + 1 + CREDIT["pv_sb"]))
                for i in range(TILES):
                    last = pe.transpose(nt_bank[g][:, P * i:P * i + P], ou[:, g % 2, P * i:P * i + P], ident[:])
                last.then_inc(nt_psum, 1)

            def att_transposes(c, t):
                pe.wait_ge(att_done, GROUPS * c + 2 * t + 2)
                for i in range(TILES):
                    last = pe.transpose((work[1], mx_bank[2])[t][:, P * i:P * i + P], att[:, i, P * t:P * t + P], ident[:])
                last.then_inc(at_psum, 1)

            def out_project(c, u, k):
                if k:
                    pe.wait_ge(at_sb, DT * c + DT)
                for i in range(2):
                    q0 = P * (2 * u + i)
                    last = pe.matmul(work[u][:, DIM * i:DIM * i + DIM], att_t[:, k, q0:q0 + P], wo[:, k, :],
                                     start=(k == 0 and i == 0), stop=bool(k), skip_group_check=True)
                if k:
                    last.then_inc(o_psum, 1)

            def v_project(b, tiles=range(3)):
                for tile in tiles:
                    m = TILE_ROWS[tile]
                    if b:
                        pe.wait_ge(v_step, 4 * (b - 1) + (1, 3, 4)[tile])
                    keys = ctx2[:, :, b, :, :].rearrange("p t r k -> p t (r k)")
                    for k in range(DT):
                        last = pe.matmul(v_banks[tile][0:m, 0:DIM], keys[:, k, ROWS * tile:ROWS * tile + m], wv[:, k, :],
                                         start=(k == 0), stop=(k == DT - 1))
                    last.then_inc(v_psum, 1)

            def k_project(t):
                for half in range(2):
                    if t:
                        pe.wait_ge(k_step, half + 1)
                    for k in range(DT):
                        last = pe.matmul(st_bank[half][:, 0:PAIR_KEYS], wk[:, k, P * t:P * t + P],
                                         ctx2[:, k, 2 * half:2 * half + 2, 0, :], start=(k == 0), stop=(k == DT - 1))
                    last.then_inc(k_psum, 1)

            def first_maxes(m0, m1):
                for m in range(m0, m1):
                    if m % (MX // DT) == 0:
                        pe.wait_ge(k_stacked[m // (MX // DT)], 16 * K_STACK_DMAS)
                        pe.wait_ge(mask_rows, m // (MX // DT) + 1)
                    max_scores(0, 0, 0, m)

            pe.wait_ge(k_params, 64)
            k_project(0)
            pe.wait_ge(pool_init, 4)
            for t in range(DT):
                x_transposes(0, t)
            pe.wait_ge(wq_split, 1)
            q_project(0, 0)
            k_project(1)
            q_project(0, 1)
            pe.wait_ge(v_params, 48)
            pe.wait_ge(k_step, 5)
            v_project(0)
            v_project(1)
            pe.wait_ge(fixed_rows, 16 * FIXED_ROW_DMAS)
            first_maxes(0, 12)
            pe.wait_ge(q_lo_done, DT)
            x_transposes(1, 0)
            first_maxes(12, 14)
            x_transposes(1, 1)
            first_maxes(14, 16)
            v_project(2, [0])
            first_maxes(16, 18)
            for t in range(DT):
                for k in range(DT):
                    q_project(1, t, [k])
                    first_maxes(18 + 2 * (DT * t + k), 20 + 2 * (DT * t + k))
            v_project(2, [1])
            first_maxes(26, 28)
            v_project(2, [2])
            first_maxes(28, MX)
            max_transposes(0)
            v_project(3)
            pe.wait_ge(v_step, 4 * BATCH)
            pe.wait_ge(bv_ready, 1)
            pe.wait_ge(wo_ready, 1)
            for k in range(DT):
                last = pe.matmul(pv_bank[:, 0:DIM], bv_wide[:, k, :], wo[:, k, :], start=(k == 0), stop=(k == DT - 1))
            last.then_inc(bo_psum, 1)
            for i in range(ST_PER_GROUP):
                scores(0, 0, 0, i)
            pe.wait_ge(mxt_sb, 1)
            pe.wait_ge(bo_ready, 1)
            pe.wait_ge(zeroed, 3)

            def chunk(c, b, j):
                n, nb, nj = c + 1, (b if j == 0 else b + 1), 1 - j
                last_chunk = peeled(b) and j == PER_BATCH - 1
                for g in range(1, GROUPS):
                    i = ST_PER_GROUP * g
                    m0, m1 = MX_STEPS[g - 1], MX_STEPS[g]
                    order = list(range(m0, m1))

                    def maxes(count):
                        for _ in range(count):
                            if order and not last_chunk:
                                max_scores(n, nb, nj, order.pop(0))

                    for s in range(2):
                        scores(c, b, j, i + 2 * s)
                        maxes(1)
                        scores(c, b, j, i + 2 * s + 1)
                        maxes(1)
                        values(c, b, g - 1, s)
                        maxes(2)
                    scores(c, b, j, i + 4)
                    maxes(1)
                    scores(c, b, j, i + 5)
                    maxes(1)
                    if g >= 2:
                        pe.wait_ge(x1_done, 2 * c + (g - 3 + CREDIT["x1_done"]))
                        norm_transposes(c, g - 2)
                    maxes(MX)
                pe.wait_ge(att_done, GROUPS * c + 1)
                norm_transposes(c, 2)
                values(c, b, GROUPS - 1, 0)
                if not last_chunk:
                    max_transposes(n)
                if not peeled(b):
                    for t in range(DT):
                        x_transposes(c + 2, t)
                att_transposes(c, 0)
                values(c, b, GROUPS - 1, 1)
                if not peeled(b):
                    pe.wait_ge(att_done, GROUPS * c + 3)
                    q_project(c + 2, 0)
                    scores(n, nb, nj, 0)
                    scores(n, nb, nj, 1)
                    pe.wait_ge(at_sb, DT * c + 1)
                    q_project(c + 2, 1)
                    norm_transposes(c, 3)
                    scores(n, nb, nj, 2)
                    scores(n, nb, nj, 3)
                    pe.wait_ge(q_lo_done, DT * (c + 2) + 1)
                    out_project(c, 0, 0)
                    scores(n, nb, nj, 4)
                    scores(n, nb, nj, 5)
                    att_transposes(c, 1)
                    pe.wait_ge(q_lo_done, DT * (c + 2) + 2)
                    out_project(c, 1, 0)
                    out_project(c, 0, 1)
                    out_project(c, 1, 1)
                    return
                if last_chunk:
                    pe.wait_ge(wide_found, 2)
                    pe.matmul(mx_bank[0][0:1, 0:2], ones_col[:], w_wide[:], start=True,
                              stop=True).then_inc(wide_counted, 1)
                    for t in range(DT):
                        x_transposes(CHUNKS, t)
                norm_transposes(c, 3)
                pe.wait_ge(att_done, GROUPS * c + 3)
                pe.wait_ge(at_sb, DT * c + 1)
                out_project(c, 0, 0)
                att_transposes(c, 1)
                if not last_chunk:
                    scores(n, nb, nj, 0)
                    scores(n, nb, nj, 1)
                out_project(c, 1, 0)
                if not last_chunk:
                    scores(n, nb, nj, 2)
                out_project(c, 0, 1)
                if not last_chunk:
                    scores(n, nb, nj, 3)
                    scores(n, nb, nj, 4)
                out_project(c, 1, 1)
                if not last_chunk:
                    scores(n, nb, nj, 5)

            all_chunks(pe, chunk)


def feed_forward(nc, st, sb, sem, out_rows, x_sb, ident, ffn_gate, wi_gu, wi_d, stats, mean_var,
                 var_eps, eps, minus_half, rstd, xh, xh_t):
    def f_sb(name, shape, dtype=F32):
        return sb(name, shape, dtype, st)

    def f_sem(name):
        return sem(name, st)

    w_gu = f_sb("w_gu", [P, DT, 2, HIDDEN])
    w_d = f_sb("w_d", [P, HT, DIM])
    waiter = f_sb("f_waiter", [P, 1])
    silu = f_sb("silu", [P, 2, CHUNK])
    hidden = f_sb("hidden", [P, 2, HT, CHUNK])

    def bank(name):
        return st.enter_context(nc.psum_tensor(name, [P, 512], F32))

    xt_bank = [bank(f"xt_bank{i}") for i in range(2)]
    gate_bank = [bank(f"gate_bank{i}") for i in range(2)]
    up_bank = [bank(f"up_bank{i}") for i in range(2)]
    down_bank = [bank(f"down_bank{i}") for i in range(2)]

    w_ready = f_sem("w_ready")
    stats_step = f_sem("f_stats_step")
    stats_done = f_sem("f_stats_done")
    pool_step = f_sem("f_pool_step")
    normed = f_sem("f_normed")
    xt_psum = f_sem("f_xt_psum")
    xt_sb = f_sem("f_xt_sb")
    gate_psum = f_sem("gate_psum")
    up_psum = f_sem("up_psum")
    silu_done = f_sem("silu_done")
    hidden_done = f_sem("hidden_done")
    down_psum = f_sem("down_psum")
    y_done = f_sem("y_done")
    stored = f_sem("stored")

    Y_CREDIT = 2

    def loop(engine, chunk):
        chunk(0, 0)
        with engine.Fori(0, (CHUNKS - 2) // 2) as i:
            for j in range(2):
                chunk(2 * i + 1 + j, 1 - j)
        chunk(CHUNKS - 1, (CHUNKS - 1) % 2)

    with nc.Block() as block:

        @block.sync
        def _(sp):
            def chunk(c, parity):
                sp.wait_ge(y_done, 2 * c + (2 + Y_CREDIT))
                rows = bass.ds(TILES * c, TILES)
                sp.dma_start(out_rows[:, rows, :], x_sb[:, rows, :]).then_inc(stored, 16)
            loop(sp, chunk)
            sp.wait_ge(stored, 16 * CHUNKS)

        @block.gpsimd
        def _(pool):
            pool.sem_inc(pool_step, 2)
            with pool.Fori(0, CHUNKS - 1) as c:
                inverse_deviation(pool, c + 1, stats_done, pool_step, var_eps, mean_var, eps, minus_half, rstd)

        @block.scalar
        def _(act):
            act.activation(w_gu[:], wi_gu[:], ACT.Copy, scale=WEIGHT_SCALE).then_inc(w_ready, 1)

            act.sem_inc(xt_sb, DT)

            def chunk(c, parity):
                for t in range(DT):
                    if first(c):
                        break
                    act.wait_ge(xt_psum, DT * c + t + 1)
                    if t == 0:
                        act.wait_ge(up_psum, HT * c)
                    act.copy(xh_t[:, t, :], xt_bank[t][:, :]).then_inc(xt_sb, 1)
                for h in range(HT):
                    act.wait_ge(gate_psum, HT * c + h + 1)
                    if not (first(c) and h < 2):
                        act.wait_ge(hidden_done, HT * c + h - 1)
                    act.activation(silu[:, h % 2, :], gate_bank[h % 2][:, :], ACT.Silu).then_inc(silu_done, 1)
            loop(act, chunk)

        @block.vector
        def _(dve):
            dve.sem_inc(y_done, Y_CREDIT)
            for done in (stats_step, stats_done, normed):
                dve.sem_inc(done, 1)
            dve.tensor_scalar(w_d[:], wi_d[:], WEIGHT_SCALE, None, ALU.mult).then_inc(w_ready, 1)

            def chunk_stats(n):
                row_stats(dve, n, x_sb, stats, mean_var, stats_step, stats_done, normed, waiter)

            def chunk_norm(n):
                normalise_rows(dve, n, x_sb, xh, mean_var, rstd, pool_step, xt_psum, normed)

            def residual(c, u):
                dve.wait_ge(down_psum, 2 * c + u + 1)
                rows = x_sb[:, bass.ds(TILES * c + 2 * u, 2), :]
                dve.scalar_tensor_tensor(rows, down_bank[u][:, :].rearrange("q (t d) -> q t d", t=2),
                                         ffn_gate[:, 0:1], rows, ALU.mult, ALU.add).then_inc(y_done, 1)

            def chunk(c, parity):
                last_chunk = isinstance(c, int) and c == CHUNKS - 1
                if not last_chunk:
                    chunk_stats(c + 1)
                    chunk_norm(c + 1)
                for h in range(HT):
                    dve.wait_ge(up_psum, HT * c + h + 1)
                    dve.wait_ge(silu_done, HT * c + h + 1)
                    dve.tensor_tensor(hidden[:, parity, h, :], up_bank[h % 2][:, :], silu[:, h % 2, :],
                                      ALU.mult).then_inc(hidden_done, 1)
                    if h == 2 and not first(c):
                        for u in range(2):
                            residual(c - 1, u)
                if last_chunk:
                    for u in range(2):
                        residual(c, u)
            loop(dve, chunk)

        @block.tensor
        def _(pe):
            pe.wait_ge(w_ready, 2)

            def x_transposes(n):
                if not first(n):
                    pe.wait_ge(normed, n + 1)
                for t in range(DT):
                    if not first(n):
                        pe.wait_ge(xt_sb, DT * n)
                    for i in range(TILES):
                        last = pe.transpose(xt_bank[t][:, P * i:P * i + P], xh[:, i, P * t:P * t + P], ident[:])
                    last.then_inc(xt_psum, 1)

            def gate_up(c, h):
                if not (first(c) and h < 2):
                    pe.wait_ge(hidden_done, HT * c + h - 1)
                for which, (banks, done) in enumerate(((gate_bank, gate_psum), (up_bank, up_psum))):
                    for k in range(DT):
                        last = pe.matmul(banks[h % 2][:, :], w_gu[:, k, which, P * h:P * h + P], xh_t[:, k, :],
                                         start=(k == 0), stop=(k == DT - 1))
                    last.then_inc(done, 1)

            def down(c, parity, u):
                pe.wait_ge(hidden_done, HT * c + HT)
                pe.wait_ge(y_done, 2 * c + (u - 1 + Y_CREDIT))
                for i in range(2):
                    q0 = P * (2 * u + i)
                    for h in range(HT):
                        last = pe.matmul(down_bank[u][:, DIM * i:DIM * i + DIM], hidden[:, parity, h, q0:q0 + P],
                                         w_d[:, h, :], start=(h == 0), stop=(h == HT - 1))
                last.then_inc(down_psum, 1)

            pe.sem_inc(xt_psum, DT)

            def chunk(c, parity):
                pe.wait_ge(xt_sb, DT * c + DT)
                for h in range(HT):
                    gate_up(c, h)
                    if h == 1 and not first(c):
                        for u in range(2):
                            down(c - 1, 1 - parity, u)
                if isinstance(c, int) and c == CHUNKS - 1:
                    for u in range(2):
                        down(c, parity, u)
                else:
                    x_transposes(c + 1)
            loop(pe, chunk)


def feed_forward_narrow(nc, st, sb, sem, out_rows, x_sb, ident, ffn_gate, w_gu, w_d, stats, mean_var,
                        var_eps, eps, minus_half, rstd, xh, xt_hi, xt_lo):
    def f_sb(name, shape, dtype=F32):
        return sb("n_" + name, shape, dtype, st)

    def f_sem(name):
        return sem("n_" + name, st)

    waiter = f_sb("waiter", [P, 1])
    silu = f_sb("silu", [P, 2, CHUNK])
    hidden = f_sb("hidden", [P, 2, CHUNK])
    h_hi = f_sb("h_hi", [P, 2, HT, CHUNK], F16)
    h_lo = f_sb("h_lo", [P, 2, HT, CHUNK], F16)
    out_gate = f_sb("out_gate", [P, 1])

    def bank(name):
        return st.enter_context(nc.psum_tensor("n_" + name, [P, 512], F32))

    xt_bank = [bank(f"xt_bank{i}") for i in range(2)]
    gate_bank = [bank(f"gate_bank{i}") for i in range(2)]
    up_bank = [bank(f"up_bank{i}") for i in range(2)]
    down_bank = [bank(f"down_bank{i}") for i in range(2)]

    gate_ready = f_sem("gate_ready")
    stats_step = f_sem("stats_step")
    stats_done = f_sem("stats_done")
    pool_step = f_sem("pool_step")
    normed = f_sem("normed")
    xt_psum = f_sem("xt_psum")
    xt_hi_done = f_sem("xt_hi_done")
    xt_lo_done = f_sem("xt_lo_done")
    gate_psum = f_sem("gate_psum")
    up_psum = f_sem("up_psum")
    silu_done = f_sem("silu_done")
    hidden_done = f_sem("hidden_done")
    h_hi_done = f_sem("h_hi_done")
    h_lo_done = f_sem("h_lo_done")
    down_psum = f_sem("down_psum")
    y_done = f_sem("y_done")
    stored = f_sem("stored")

    Y_CREDIT = 2

    def turn(c):
        return 3 if first(c) else 2

    def loop(engine, chunk):
        chunk(0, 0)
        with engine.Fori(0, (CHUNKS - 2) // 2) as i:
            for j in range(2):
                chunk(2 * i + 1 + j, 1 - j)
        chunk(CHUNKS - 1, (CHUNKS - 1) % 2)

    with nc.Block() as block:

        @block.sync
        def _(sp):
            with sp.Fori(0, CHUNKS - 1) as c:
                sp.wait_ge(y_done, 2 * c + (2 + Y_CREDIT))
                rows = bass.ds(TILES * c, TILES)
                sp.dma_start(out_rows[:, rows, :], x_sb[:, rows, :]).then_inc(stored, 16)
            for u in range(2):
                sp.wait_ge(y_done, 2 * (CHUNKS - 1) + u + 1 + Y_CREDIT)
                rows = bass.ds(TILES * (CHUNKS - 1) + u * (TILES // 2), TILES // 2)
                sp.dma_start(out_rows[:, rows, :], x_sb[:, rows, :]).then_inc(stored, 16)
            sp.wait_ge(stored, 16 * (CHUNKS + 1))

        @block.gpsimd
        def _(pool):
            pool.sem_inc(pool_step, 2)
            with pool.Fori(0, CHUNKS - 1) as c:
                inverse_deviation(pool, c + 1, stats_done, pool_step, var_eps, mean_var, eps, minus_half, rstd)

        @block.scalar
        def _(act):
            act.sem_inc(xt_hi_done, DT)
            act.mul(out_gate[:], ffn_gate[:], WEIGHT_SCALE / HIDDEN_SCALE).then_inc(gate_ready, 1)

            def x_high(n, parity):
                for t in range(DT):
                    act.wait_ge(xt_psum, DT * n + t + 1)
                    if not (isinstance(n, int) and n < 2) and t == 0:
                        act.wait_ge(up_psum, HT * (n - 1))
                    act.activation(xt_hi[:, parity, t, :], xt_bank[t][:, :], ACT.Copy, scale=X_SCALE).then_inc(xt_hi_done, 1)

            def high(c, parity, h):
                act.wait_ge(hidden_done, HT * c + h + 1)
                if h == 0 and not (isinstance(c, int) and c < 2):
                    act.wait_ge(down_psum, 2 * (c - 1))
                act.copy(h_hi[:, parity, h, :], hidden[:, h % 2, :]).then_inc(h_hi_done, 1)

            def chunk(c, parity):
                for h in range(HT):
                    act.wait_ge(gate_psum, HT * c + h + 1)
                    if not (first(c) and h < 2):
                        act.wait_ge(hidden_done, HT * c + h - 1)
                    act.activation(silu[:, h % 2, :], gate_bank[h % 2][:, :], ACT.Silu,
                                   scale=WEIGHT_SCALE / X_SCALE).then_inc(silu_done, 1)
                    if h >= 1:
                        high(c, parity, h - 1)
                    if h == turn(c) and not (isinstance(c, int) and c == CHUNKS - 1):
                        x_high(c + 1, 1 - parity)
                high(c, parity, HT - 1)
            loop(act, chunk)

        @block.vector
        def _(dve):
            dve.sem_inc(y_done, Y_CREDIT)
            for done in (stats_step, stats_done, normed):
                dve.sem_inc(done, 1)
            dve.sem_inc(xt_lo_done, DT)

            def chunk_stats(n):
                row_stats(dve, n, x_sb, stats, mean_var, stats_step, stats_done, normed, waiter)

            def chunk_norm(n):
                normalise_rows(dve, n, x_sb, xh, mean_var, rstd, pool_step, xt_psum, normed)

            def x_low(n, parity):
                for t in range(DT):
                    dve.wait_ge(xt_hi_done, DT * n + t + 1)
                    dve.scalar_tensor_tensor(xt_lo[:, parity, t, :], xt_bank[t][:, :], X_SCALE, xt_hi[:, parity, t, :],
                                             ALU.mult, ALU.subtract).then_inc(xt_lo_done, 1)

            def low(c, parity, h):
                dve.wait_ge(h_hi_done, HT * c + h + 1)
                dve.tensor_tensor(h_lo[:, parity, h, :], hidden[:, h % 2, :], h_hi[:, parity, h, :],
                                  ALU.subtract).then_inc(h_lo_done, 1)

            def residual(c, u):
                dve.wait_ge(down_psum, 2 * c + u + 1)
                rows = x_sb[:, bass.ds(TILES * c + 2 * u, 2), :]
                dve.scalar_tensor_tensor(rows, down_bank[u][:, :].rearrange("q (t d) -> q t d", t=2),
                                         out_gate[:, 0:1], rows, ALU.mult, ALU.add).then_inc(y_done, 1)

            dve.wait_ge(gate_ready, 1)
            chunk_stats(1)

            def chunk(c, parity):
                last_chunk = isinstance(c, int) and c == CHUNKS - 1
                for h in range(HT):
                    dve.wait_ge(up_psum, HT * c + h + 1)
                    dve.wait_ge(silu_done, HT * c + h + 1)
                    if not (first(c) and h < 2):
                        dve.wait_ge(h_lo_done, HT * c + h - 1)
                    dve.scalar_tensor_tensor(hidden[:, h % 2, :], up_bank[h % 2][:, :],
                                             HIDDEN_SCALE * WEIGHT_SCALE / X_SCALE, silu[:, h % 2, :],
                                             ALU.mult, ALU.mult).then_inc(hidden_done, 1)
                    if h == 0 and not last_chunk and not first(c):
                        chunk_stats(c + 1)
                    if h >= 1:
                        low(c, parity, h - 1)
                    if h == 1 and not last_chunk:
                        chunk_norm(c + 1)
                    start = 2 if last_chunk else 3
                    if h in (start, start + 1) and not first(c):
                        residual(c - 1, h - start)
                    if h == turn(c) and not last_chunk:
                        x_low(c + 1, 1 - parity)
                low(c, parity, HT - 1)
                if last_chunk:
                    for u in range(2):
                        residual(c, u)
            loop(dve, chunk)

        @block.tensor
        def _(pe):
            def x_transposes(n):
                if not first(n):
                    pe.wait_ge(normed, n + 1)
                for t in range(DT):
                    if not first(n):
                        pe.wait_ge(xt_lo_done, DT * n)
                    for i in range(TILES):
                        last = pe.transpose(xt_bank[t][:, P * i:P * i + P], xh[:, i, P * t:P * t + P], ident[:])
                    last.then_inc(xt_psum, 1)

            def gate_up(c, parity, h):
                if not (first(c) and h < 2):
                    pe.wait_ge(hidden_done, HT * c + h - 1)
                for which, (banks, done) in enumerate(((gate_bank, gate_psum), (up_bank, up_psum))):
                    for part in (xt_hi, xt_lo):
                        for k in range(DT):
                            last = pe.matmul(banks[h % 2][:, :], w_gu[:, k, which, P * h:P * h + P], part[:, parity, k, :],
                                             start=(part is xt_hi and k == 0), stop=(part is xt_lo and k == DT - 1))
                    last.then_inc(done, 1)

            def down(c, parity, u):
                pe.wait_ge(y_done, 2 * c + (u - 1 + Y_CREDIT))
                for i in range(2):
                    q0 = P * (2 * u + i)
                    for h in range(HT):
                        if u == 0 and i == 0:
                            pe.wait_ge(h_lo_done, HT * c + h + 1)
                        for part in (h_hi, h_lo):
                            last = pe.matmul(down_bank[u][:, DIM * i:DIM * i + DIM], part[:, parity, h, q0:q0 + P],
                                             w_d[:, h, :], start=(h == 0 and part is h_hi),
                                             stop=(h == HT - 1 and part is h_lo))
                last.then_inc(down_psum, 1)

            pe.sem_inc(xt_psum, DT)

            def chunk(c, parity):
                last_chunk = isinstance(c, int) and c == CHUNKS - 1
                pe.wait_ge(xt_hi_done, DT * c + DT)
                pe.wait_ge(xt_lo_done, DT * c + DT)
                for h in range(HT):
                    gate_up(c, parity, h)
                    if h == turn(c) and not last_chunk:
                        x_transposes(c + 1)
                    if h in (1, 2) and not first(c):
                        down(c - 1, 1 - parity, h - 1)
                if last_chunk:
                    for u in range(2):
                        down(c, parity, u)
            loop(pe, chunk)


def kernel(**inputs):
    import numpy as _np
    import concourse.bacc as _bacc
    from concourse import mybir as _mybir
    from concourse.bass_utils import run_bass_kernel_spmd as _run

    a = {k: _np.asarray(v) for k, v in inputs.items()}
    ctx = a["ctx_1024"]
    laid_out = {
        "x": a["x"],
        "ctx_t": ctx.reshape(-1, ctx.shape[-1]).T,
        "mask": a["mask_BxS2_bk0"],
        "g_xattn": a["g_xattn"],
        "g_ffn": a["g_ffn"],
        "w_q": a["L0_xattn_W_Q"], "b_q": a["L0_xattn_b_Q"].reshape(DT, P).T,
        "w_k": a["L0_xattn_W_K"], "b_k": a["L0_xattn_b_K"].reshape(DT, P).T,
        "w_v": a["L0_xattn_W_V"], "b_v": a["L0_xattn_b_V"].reshape(DT, P).T,
        "w_o": a["L0_xattn_W_O"], "b_o": a["L0_xattn_b_O"],
        "w_gate_t": a["L0_ffn_w_gate"].T,
        "w_up_t": a["L0_ffn_w_up"].T,
        "w_down_t": a["L0_ffn_w_down"].T,
    }
    nc = _bacc.Bacc("TRN2", target_bir_lowering=False, num_devices=1)
    arrays, args = {}, []
    for name, value in laid_out.items():
        value = _np.ascontiguousarray(value)
        arrays[f"in_{name}_dram"] = value
        args.append(nc.dram_tensor(f"in_{name}_dram", value.shape, _mybir.dt.from_np(value.dtype), kind="ExternalInput").ap())
    out = nc.dram_tensor("out_0_dram", a["x"].shape, _mybir.dt.float32, kind="ExternalOutput").ap()
    flamingo_block(nc, *args, out)
    r = _run(nc, [arrays], core_ids=[0])
    return r.results[0]["out_0_dram"]
```
